# Optimizing a Trainium2 kernel written in Bass

```python
import numpy as np
import jax
import jax.numpy as jnp

def _softmax(x, axis=-1):
    return jax.nn.softmax(x, axis=axis)

def _gelu(x):
    return jax.nn.gelu(x, approximate=True)

def _silu(x):
    return jax.nn.silu(x)

def _sigmoid(x):
    return jax.nn.sigmoid(x)

def _layernorm(x, axis=-1, eps=1e-05):
    m = jnp.mean(x, axis=axis, keepdims=True)
    v = jnp.var(x, axis=axis, keepdims=True)
    return (x - m) / jnp.sqrt(v + eps)

def _scatter_add(tgt, idx, src, axis=0):
    return tgt.at[idx].add(src)

def _segment_sum(src, seg, n):
    return jax.ops.segment_sum(src, seg, n)
kernel_name = 'mk_conv_preact_d2_conv_nchw128_r2_2afbbf'

def setup_inputs(seed: int=0):
    np.random.seed(seed)
    _w = jnp.asarray

    def _rec_inputs():
        import jax
        import jax.numpy as jnp
        _gk = jax.random.key(seed)
        x = 7.22e-05 + 1 * jax.random.normal(jax.random.fold_in(_gk, 1), (16, 64, 32, 32), jnp.float32)
        return x
    x = _rec_inputs()

    def _L0_conv_setup():
        import jax, jax.numpy as jnp
        import numpy as np
        NUM_HEADS = 4
        HEAD_DIM = 32
        EPS = 1e-05
        key = jax.random.key(seed)
        k1, k2, k3 = jax.random.split(key, 3)
        B, C, H, W = (16, 64, 32, 32)
        hidden = NUM_HEADS * HEAD_DIM
        x = jax.random.normal(k1, (B, C, H, W), dtype=jnp.float32)
        w_qkv = jax.random.normal(k2, (3 * hidden, C), dtype=jnp.float32) * (1.0 / np.sqrt(C))
        w_out = jax.random.normal(k3, (C, hidden), dtype=jnp.float32) * (1.0 / np.sqrt(hidden))
        b_out = jnp.zeros((C,), dtype=jnp.float32)
        gn_weight = jnp.ones((C,), dtype=jnp.float32)
        gn_bias = jnp.zeros((C,), dtype=jnp.float32)
        return {'x': x, 'w_qkv': w_qkv, 'w_out': w_out, 'b_out': b_out, 'gn_weight': gn_weight, 'gn_bias': gn_bias}
    _L0_conv_all = _L0_conv_setup()
    _L0_conv_in = {k: v for k, v in _L0_conv_all.items() if k in ('w_qkv', 'w_out', 'b_out', 'gn_weight', 'gn_bias')}
    del _L0_conv_all

    def _L1_conv_setup():
        import jax, jax.numpy as jnp
        import numpy as np
        K = 9
        GROUPS = 4
        EPS_GN = 1e-05

        def group_norm(x, gamma, beta):
            B, C, H, W = x.shape
            xg = x.reshape(B, GROUPS, -1)
            mu = xg.mean(axis=-1, keepdims=True)
            var = xg.var(axis=-1, keepdims=True)
            xn = ((xg - mu) / jnp.sqrt(var + EPS_GN)).reshape(B, C, H, W)
            return xn * gamma[None, :, None, None] + beta[None, :, None, None]
        key = jax.random.key(seed)
        ks = jax.random.split(key, 6)
        B, C, H, W = (32, 64, 45, 45)
        std = 1.0 / np.sqrt(C)
        x = jax.random.normal(ks[0], (B, C, H, W), dtype=jnp.float32)
        w1 = jax.random.uniform(ks[1], (C, C), jnp.float32, -std, std)
        b1 = jax.random.uniform(ks[2], (C,), jnp.float32, -std, std)
        w2 = jax.random.uniform(ks[3], (C, C), jnp.float32, -std, std)
        b2 = jax.random.uniform(ks[4], (C,), jnp.float32, -std, std)
        gamma1 = jnp.ones((C,), jnp.float32)
        beta1 = jnp.zeros((C,), jnp.float32)
        gamma2 = jnp.ones((C,), jnp.float32)
        beta2 = jnp.zeros((C,), jnp.float32)
        return {'x': x, 'w1': w1, 'b1': b1, 'w2': w2, 'b2': b2, 'gamma1': gamma1, 'beta1': beta1, 'gamma2': gamma2, 'beta2': beta2}
    _L1_conv_all = _L1_conv_setup()
    _L1_conv_in = {k: v for k, v in _L1_conv_all.items() if k in ('w1', 'b1', 'w2', 'b2', 'gamma1', 'beta1', 'gamma2', 'beta2')}
    del _L1_conv_all
    return {'x': x, 'L0_conv_w_qkv': _L0_conv_in['w_qkv'], 'L0_conv_w_out': _L0_conv_in['w_out'], 'L0_conv_b_out': _L0_conv_in['b_out'], 'L0_conv_gn_weight': _L0_conv_in['gn_weight'], 'L0_conv_gn_bias': _L0_conv_in['gn_bias'], 'L1_conv_w1': _L1_conv_in['w1'], 'L1_conv_b1': _L1_conv_in['b1'], 'L1_conv_w2': _L1_conv_in['w2'], 'L1_conv_b2': _L1_conv_in['b2'], 'L1_conv_gamma1': _L1_conv_in['gamma1'], 'L1_conv_beta1': _L1_conv_in['beta1'], 'L1_conv_gamma2': _L1_conv_in['gamma2'], 'L1_conv_beta2': _L1_conv_in['beta2']}

def reference(x, L0_conv_w_qkv, L0_conv_w_out, L0_conv_b_out, L0_conv_gn_weight, L0_conv_gn_bias, L1_conv_w1, L1_conv_b1, L1_conv_w2, L1_conv_b2, L1_conv_gamma1, L1_conv_beta1, L1_conv_gamma2, L1_conv_beta2):
    import jax
    import jax.numpy as jnp

    def _L0_conv_ref(x, w_qkv, w_out, b_out, gn_weight, gn_bias):
        import jax, jax.numpy as jnp
        import numpy as np
        NUM_HEADS = 4
        HEAD_DIM = 32
        EPS = 1e-05
        B, C, H, W = x.shape
        N = H * W
        scale = HEAD_DIM ** (-0.5)
        qkv = jnp.einsum('oc,bcn->bon', w_qkv, x.reshape(B, C, N))
        qkv = qkv.reshape(B, 3, NUM_HEADS, HEAD_DIM, N)
        q, k, v = (qkv[:, 0], qkv[:, 1], qkv[:, 2])
        q = jax.nn.softmax(q, axis=-2) * scale
        k = jax.nn.softmax(k, axis=-1)
        context = jnp.einsum('bhdn,bhen->bhde', k, v)
        out = jnp.einsum('bhde,bhdn->bhen', context, q)
        out = out.reshape(B, NUM_HEADS * HEAD_DIM, N)
        out = jnp.einsum('oc,bcn->bon', w_out, out) + b_out[None, :, None]
        mean = out.mean(axis=(1, 2), keepdims=True)
        var = out.var(axis=(1, 2), keepdims=True)
        out = (out - mean) * jax.lax.rsqrt(var + EPS)
        out = out * gn_weight[None, :, None] + gn_bias[None, :, None]
        return out.reshape(B, C, H, W)

    def _L1_conv_ref(x, w1, b1, w2, b2, gamma1, beta1, gamma2, beta2):
        import jax, jax.numpy as jnp
        import numpy as np
        K = 9
        GROUPS = 4
        EPS_GN = 1e-05

        def group_norm(x, gamma, beta):
            B, C, H, W = x.shape
            xg = x.reshape(B, GROUPS, -1)
            mu = xg.mean(axis=-1, keepdims=True)
            var = xg.var(axis=-1, keepdims=True)
            xn = ((xg - mu) / jnp.sqrt(var + EPS_GN)).reshape(B, C, H, W)
            return xn * gamma[None, :, None, None] + beta[None, :, None, None]
        B, C, H, W = x.shape
        N = H * W
        xf = x.reshape(B, C, N).transpose(0, 2, 1)
        nrm = jnp.linalg.norm(xf, axis=-1, keepdims=True)
        xn = xf / jnp.maximum(nrm, 1e-12)
        sim = jnp.einsum('bnc,bmc->bnm', xn, xn)
        val, idx = jax.lax.top_k(sim, K)
        v = val / (val.sum(axis=-1, keepdims=True) + 1e-06)

        def gcn_apply(feat, w, b):
            xt = feat @ w
            neigh = jax.vmap(lambda t, i: t[i])(xt, idx)
            return jnp.einsum('bnkc,bnk->bnc', neigh, v) + b
        out = gcn_apply(xn, w1, b1)
        out = jax.nn.silu(group_norm(out.transpose(0, 2, 1).reshape(B, C, H, W), gamma1, beta1))
        of = out.reshape(B, C, N).transpose(0, 2, 1)
        out = gcn_apply(of, w2, b2)
        out = jax.nn.silu(group_norm(out.transpose(0, 2, 1).reshape(B, C, H, W), gamma2, beta2))
        return out

    def _gn(v, G=32, eps=1e-05):
        B_, C_, H_, W_ = v.shape
        g = v.reshape(B_, G, C_ // G, H_, W_)
        m = jnp.mean(g, axis=(2, 3, 4), keepdims=True)
        s = jnp.var(g, axis=(2, 3, 4), keepdims=True)
        return ((g - m) / jnp.sqrt(s + eps)).reshape(v.shape)

    def _ln_c(v, eps=1e-06):
        m = jnp.mean(v, axis=1, keepdims=True)
        s = jnp.var(v, axis=1, keepdims=True)
        return (v - m) / jnp.sqrt(s + eps)

    def _ln_t(v, eps=1e-05):
        m = jnp.mean(v, axis=-1, keepdims=True)
        s = jnp.var(v, axis=-1, keepdims=True)
        return (v - m) / jnp.sqrt(s + eps)

    def _to_tokens(v):
        B_, C_, H_, W_ = v.shape
        return v.reshape(B_, C_, H_ * W_).transpose(0, 2, 1)

    def _from_tokens(t, like):
        B_, C_, H_, W_ = like.shape
        return t.transpose(0, 2, 1).reshape(B_, C_, H_, W_)
    x = x + _L0_conv_ref(_gn(x), L0_conv_w_qkv, L0_conv_w_out, L0_conv_b_out, L0_conv_gn_weight, L0_conv_gn_bias)
    x = x + _L1_conv_ref(_gn(x), L1_conv_w1, L1_conv_b1, L1_conv_w2, L1_conv_b2, L1_conv_gamma1, L1_conv_beta1, L1_conv_gamma2, L1_conv_beta2)
    return x

_drawn_inputs = setup_inputs


def setup_inputs(seed=0):
    import zlib

    import numpy as np

    out = dict(_drawn_inputs(seed))
    spreads = {'L0_conv_b_out': (0.0, 0.1),
     'L0_conv_gn_weight': (1.0, 0.2),
     'L0_conv_gn_bias': (0.0, 0.1),
     'L1_conv_gamma1': (1.0, 0.2),
     'L1_conv_beta1': (0.0, 0.1),
     'L1_conv_gamma2': (1.0, 0.2),
     'L1_conv_beta2': (0.0, 0.1)}
    factors = {}
    for name, (base, spread) in spreads.items():
        noise = np.random.default_rng([zlib.crc32(name.encode()), seed]).standard_normal(out[name].shape)
        drawn = base * np.exp(spread * noise) if base else spread * noise
        out[name] = jnp.asarray(drawn.astype(out[name].dtype))
    for name, factor in factors.items():
        out[name] = (out[name] * factor).astype(out[name].dtype)
    return out
```

```python
from contextlib import ExitStack

import numpy as np

import concourse.bass as bass
from concourse import mybir

ALU = mybir.AluOpType
ACT = mybir.ActivationFunctionType
AX = mybir.AxisListType
F32 = mybir.dt.float32
F16 = mybir.dt.float16

P = 128
HEADS = 4
TOP = 8
XSCALE = 64.0
SSCALE = XSCALE * XSCALE
MARK = -2.5 * SSCALE
EPS = 1e-5

CONST_PARTS = [("ident", P), ("avg_pair", P), ("avg_sample", P), ("avg_group", P), ("spread", 4 * P), ("halves", 2)]
VECTORS = ["b_out", "gn_weight", "gn_bias", "b1", "gamma1", "beta1", "b2", "gamma2", "beta2"]


def column_of(parts, name):
    at = 0
    for n, width in parts:
        if n == name:
            return at, at + width
        at += width


def shape_constants(C):
    p = np.arange(P)
    channel = p % C
    out = {"ident": np.eye(P)}
    for name, size in (("avg_pair", 2), ("avg_sample", C), ("avg_group", C // 4)):
        same = channel[:, None] // size == channel[None, :] // size
        out[name] = same / same.sum(1, keepdims=True)
    spread = np.zeros((P, 4, P))
    for j in range(4):
        for q in range(P):
            spread[4 * (q // C) + j, j, q] = 1.0
    out["spread"] = spread.reshape(P, 4 * P)
    out["halves"] = np.arange(P)[:, None] // C == np.arange(2)[None, :]
    return np.concatenate([out[n] for n, _ in CONST_PARTS], axis=1).astype(np.float32)


def build(nc, x, w_q, w_k, w_v, w_o, w_1, w_2, vectors, constants, out):
    B, C, N = x.shape
    H = N // 2
    NT = N // P
    NJ = H // P
    D = P // HEADS
    SCALE = float(D) ** -0.5
    assert C == 64 and 2 * C == P and H == 512

    ctx = ExitStack()
    with ctx:
        def sb(name, shape, dt=F32):
            return ctx.enter_context(nc.sbuf_tensor(name, shape, dt))

        def sem(name):
            return ctx.enter_context(nc.semaphore(name))

        cst = sb("cst", [P, constants.shape[1]])
        vec = sb("vec", [P, vectors.shape[1]])
        wq = sb("wq", [P, P])
        wk = sb("wk", [P, P])
        wv = sb("wv", [D, HEADS, C])
        wo = sb("wo", [D, HEADS, C])
        w1r = sb("w1r", [P, C])
        w2r = sb("w2r", [P, C])
        w1 = sb("w1", [P, P])
        w2 = sb("w2", [P, P])
        u = sb("u", [C, HEADS, C])
        ident16 = sb("ident16", [P, P], F16)
        mark16 = sb("mark16", [P, P], F16)
        minus_half = sb("minus_half", [P, NT])

        def const(name):
            a, b = column_of(CONST_PARTS, name)
            return cst[:, a:b]

        def vector(name):
            i = VECTORS.index(name)
            return vec[:, i:i + 1]

        ident = const("ident")
        spread = const("spread").rearrange("p (j q) -> p j q", j=4)

        xin = [sb(f"xin{i}", [P, H]) for i in range(2)]
        y = sb("y", [P, H])
        ek = sb("ek", [P, N])
        ekT = sb("ekT", [P, NT, P])
        yT = sb("yT", [P, NJ, P])
        kyT = sb("kyT", [C, P])
        mT = sb("mT", [P, C])
        qs = sb("qs", [P, NT * HEADS, D])
        qe = sb("qe", [P, NT * HEADS, D])
        qn = sb("qn", [P, NT * HEADS, D])
        qh = sb("qh", [P, N])
        att = sb("att", [P, H])
        attn = sb("attn", [P, H])
        x1 = sb("x1", [P, H])
        y1 = sb("y1", [P, H])
        sq = sb("sq", [P, H])
        xn = [sb(f"xn{i}", [P, H]) for i in range(2)]
        xhi = sb("xhi", [P, H], F16)
        xlo = sb("xlo", [P, H], F16)
        hilo = [sb(f"hilo{i}", [P, N], F16) for i in range(2)]
        hihi = [sb(f"hihi{i}", [P, N], F16) for i in range(2)]
        lolo = [sb(f"lolo{i}", [P, N], F16) for i in range(2)]
        st = {n: sb(f"st_{n}", [P, 24]) for n in ("in", "att", "mid", "g1", "g2")}
        kstat = sb("kstat", [P, 4])
        qmax = sb("qmax", [P, NT * HEADS])
        qsum = sb("qsum", [P, NT * HEADS])
        qrec = sb("qrec", [P, NT * HEADS])
        ss = sb("ss", [P, NT])
        ssq = sb("ssq", [P, NT])
        rn = sb("rn", [P, NT])
        sn = sb("sn", [P, NT])
        selfsim = [sb(f"selfsim{i}", [P, NT]) for i in range(2)]
        rnT = sb("rnT", [NT, P])

        x1c = [sb(f"x1c{i}", [P, H]) for i in range(2)]
        xt1 = [sb(f"xt1_{i}", [P, NJ, 2, C]) for i in range(2)]
        sim = [sb(f"sim{i}", [P, N]) for i in range(2)]
        rest = [sb(f"rest{i}", [P, N]) for i in range(2)]
        adj = [sb(f"adj{i}", [P, N]) for i in range(2)]
        top = sb("top", [P, NT, TOP])
        adjT = [sb(f"adjT{i}", [P, NT, N]) for i in range(2)]
        vsum = sb("vsum", [P, NT])
        vtot = sb("vtot", [P, NT])
        vrec = [sb(f"vrec{i}", [P, NT]) for i in range(2)]

        vrT = sb("vrT", [NT, P])
        vbc = sb("vbc", [P, H])
        g = sb("g", [P, H])
        zh = sb("zh", [P, H])
        th = sb("th", [P, H])
        y2 = sb("y2", [P, H])
        xt2 = sb("xt2", [P, NJ, 2, C])
        g2 = sb("g2", [P, H])
        zh2 = sb("zh2", [P, H])
        th2 = sb("th2", [P, H])
        y3 = sb("y3", [P, H])
        res = [sb(f"res{i}", [P, H]) for i in range(2)]

        pS = ctx.enter_context(nc.psum_tensor("pS", [P, N], F32))
        pT = ctx.enter_context(nc.psum_tensor("pT", [P, NT, P], F32))
        pA = ctx.enter_context(nc.psum_tensor("pA", [P, N], F32))
        pB = ctx.enter_context(nc.psum_tensor("pB", [P, H], F32))
        pC = ctx.enter_context(nc.psum_tensor("pC", [P, H], F32))

        names = """loaded_weights prepared u_ps u_ready
            x_in0 x_in1 in_stat in_aggr in_mean_ps in_dev in_sq in_var_ps in_veps in_rstd y_ready
            k_ps k_max k_exp ek_T ekT_copied yT_ps yT_copied ky_ps ky_copied k_rec m_ps m_copied
            q_ps q_max q_sub q_exp q_sum q_rec q_norm q_T qh_copied att_ps att_copied
            att_stat att_aggr att_mean_ps att_dev att_sq att_var_ps att_veps att_rstd att_scale att_bias
            att_normed x1_ready x1_copied mid_stat mid_aggr mid_mean_ps mid_dev mid_sq mid_var_ps mid_veps
            mid_rstd y1_ready sq_ready ss_ps ss_copied rn_ready sn_ready selfsim_ready rn_T rnT_copied
            rn_spread xn_ready hi_ready lo_ready
            stacked0 stacked1 xt1_ps xt1_copied
            tile_sim_ps tile_sim tile_top tile_rest tile_marked tile_adj tile_T tile_adjT
            v_sum v_tot v_rec
            v_T vT_copied v_spread v_bc
            g1_ps g1_copied g1_stat g1_aggr g1_mean g1_mean_ps g1_dev g1_sq g1_var_ps g1_veps g1_rstd
            g1_scale g1_bias g1_half g1_tanh y2_ready xt2_ps xt2_copied
            g2_ps g2_copied g2_stat g2_aggr g2_mean g2_mean_ps g2_dev g2_sq g2_var_ps g2_veps g2_rstd
            g2_scale g2_bias g2_half g2_tanh y3_ready res_ready stored0 stored1""".split()
        done = {name: sem(name) for name in names}

        PREPARED = 9

        def since(name, count):
            if isinstance(count, int) and count <= 0:
                return done["prepared"], PREPARED
            return done[name], count

        def constant_first(eng, *counts):
            held = [count for count in counts if not isinstance(count, int)]
            for count in held:
                eng.compute_val(count)
            if held:
                eng.wait_ge(done["prepared"], PREPARED)

        def A(step):
            return 0.02 + 8.0 * step / 47

        def V(step):
            at = [0.15, 0.2, 0.25, 0.3] + [0.65 + 0.25 * k for k in range(8)] + [2.6 + 0.2 * k for k in range(8)] \
                + [4.4 + 0.25 * k for k in range(8)] + [6.4 + 0.18 * k for k in range(8)]
            k = int(step)
            return at[k] + (step - k) * 0.18

        FIRST = 3
        LATE_T = 1.6

        def weave(stages, i, par):
            attend, neighbours, convolve = stages
            known = isinstance(i, int)
            live = []
            if not known or 0 <= i < B:
                live.append(neighbours(i, par))
            if not known or 0 <= i - 1:
                live.append(convolve(i - 1, 1 - par))
            if not known or i + 1 < B:
                live.append(attend(i + 1, 1 - par))
            live = [[next(steps, None), steps] for steps in live]
            while any(at is not None for at, _ in live):
                first = min((e for e in live if e[0] is not None), key=lambda e: e[0])
                first[0] = next(first[1], None)

        def samples(eng, stages, last=1):
            for i in range(-1, FIRST):
                weave(stages, i, i % 2)
            with eng.Fori(0, (B - last - FIRST) // 2) as k:
                weave(stages, 2 * k + FIRST, 1)
                weave(stages, 2 * k + FIRST + 1, 0)
            for i in range(B - last, B + 1):
                weave(stages, i, i % 2)

        block = ctx.enter_context(nc.Block())

        @block.sync
        def _(sp):
            for dst, src in ((cst, constants), (vec, vectors), (wq, w_q), (wk, w_k), (wv, w_v), (wo, w_o),
                             (w1r, w_1), (w2r, w_2)):
                sp.dma_start(dst[:], src).then_inc(done["loaded_weights"], 16)

            def load(b, p):
                for h in range(2):
                    sp.dma_start(xin[p][h * C:(h + 1) * C, :], x[b, :, h * H:(h + 1) * H]).then_inc(done[f"x_in{p}"], 16)

            def attend(b, p):
                yield A(29.5)
                constant_first(sp, b + 1)
                sp.wait_ge(done["x1_ready"], b + 1)
                constant_first(sp, b - 1)
                sp.wait_ge(*since("res_ready", b - 1))
                sp.dma_start(x1c[p][:, :], x1[:, :]).then_inc(done["x1_copied"], 16)
                yield A(45.5)
                constant_first(sp, NT * (b - 1))
                sp.wait_ge(*since("tile_sim_ps", NT * (b - 1)))
                constant_first(sp, b + 1)
                sp.wait_ge(done["hi_ready"], b + 1)
                for h in range(2):
                    tok = slice(h * H, (h + 1) * H)
                    for dst, lo in ((hilo, 0), (hihi, 0), (hihi, C)):
                        sp.dma_start(dst[p][lo:lo + C, tok], xhi[h * C:(h + 1) * C, :]).then_inc(done[f"stacked{p}"], 16)
                yield A(46.5)
                constant_first(sp, b + 1)
                sp.wait_ge(done["lo_ready"], b + 1)
                for h in range(2):
                    tok = slice(h * H, (h + 1) * H)
                    for dst, lo in ((hilo, C), (lolo, 0), (lolo, C)):
                        sp.dma_start(dst[p][lo:lo + C, tok], xlo[h * C:(h + 1) * C, :]).then_inc(done[f"stacked{p}"], 16)

            def neighbours(b, p):
                yield 0.0
                if not isinstance(b, int) or b + 2 < B:
                    constant_first(sp, b + 1)
                    sp.wait_ge(done["x1_ready"], b + 1)
                    load(b + 2, p)

            def convolve(b, p):
                yield V(35)
                constant_first(sp, b + 1)
                sp.wait_ge(done["res_ready"], b + 1)
                for h in range(2):
                    sp.dma_start(out[b, :, h * H:(h + 1) * H], res[p][h * C:(h + 1) * C, :]).then_inc(done[f"stored{p}"], 16)

            load(0, 0)
            load(1, 1)
            samples(sp, (attend, neighbours, convolve), last=3)
            for p in range(2):
                sp.wait_ge(done[f"stored{p}"], 32 * (B // 2))

        @block.gpsimd
        def _(pool):
            pool.memset(minus_half[:, :], -0.5).then_inc(done["prepared"], 1)
            pool.memset(w1[:, :], 0.0).then_inc(done["prepared"], 1)
            pool.memset(w2[:, :], 0.0).then_inc(done["prepared"], 1)
            pool.wait_ge(done["prepared"], 3)

            def rstd(b, tag):
                pool.wait_ge(done[f"{tag}_veps"], b + 1)
                pool.tensor_tensor(st[tag][:, 13:14], st[tag][:, 12:13], minus_half[:, 0:1], ALU.pow).then_inc(done[f"{tag}_rstd"], 1)

            def attend(b, p):
                yield A(5)
                rstd(b, "in")
                yield A(16)
                pool.wait_ge(done["q_rec"], b + 1)
                pool.wait_ge(*since("q_T", b))
                pool.tensor_tensor(qn[:, :, :], qe[:, :, :], qrec[:, :].unsqueeze(2).broadcast_to([P, NT * HEADS, D]),
                                   ALU.mult).then_inc(done["q_norm"], 1)
                yield A(26)
                rstd(b, "att")
                yield A(29)
                pool.wait_ge(done["att_normed"], b + 1)
                pool.wait_ge(*since("x1_copied", 16 * b))
                pool.wait_ge(*since("y1_ready", b))
                pool.tensor_tensor(x1[:, :], attn[:, :], xin[p][:, :], ALU.add).then_inc(done["x1_ready"], 1)
                yield A(35)
                rstd(b, "mid")
                yield A(40)
                pool.wait_ge(done["ss_copied"], b + 1)
                pool.wait_ge(*since("rn_T", b))
                pool.tensor_tensor(rn[:, :], ssq[:, :], minus_half[:, :], ALU.pow).then_inc(done["rn_ready"], 1)

            def neighbours(b, p):
                for r in range(NT):
                    n = NT * b + r
                    rows = slice(r * P, (r + 1) * P)
                    yield r + 0.5
                    constant_first(pool, n + 1)
                    pool.wait_ge(done["tile_rest"], n + 1)
                    pool.affine_select(out=rest[r % 2][:, rows], in_=rest[r % 2][:, rows], compare_op=ALU.not_equal,
                                       fill=MARK, base=0, pattern=[[-1, P]], channel_multiplier=1).then_inc(done["tile_marked"], 1)
                    pool.wait_ge(done["tile_marked"], n + 1)
                    pool.wait_ge(*since("tile_T", n - 1))
                    pool.tensor_tensor(adj[r % 2][:, :], sim[r % 2][:, :], rest[r % 2][:, :], ALU.subtract).then_inc(done["tile_adj"], 1)

            def convolve(b, p):
                yield V(16)
                rstd(b, "g1")
                yield V(32)
                rstd(b, "g2")
                yield V(34)
                pool.wait_ge(done["y3_ready"], b + 1)
                pool.wait_ge(done["x1_copied"], 16 * (b + 1))
                pool.wait_ge(*since(f"stored{p}", 16 * (b - p)))
                pool.tensor_tensor(res[p][:, :], y3[:, :], x1c[p][:, :], ALU.add).then_inc(done["res_ready"], 1)

            samples(pool, (attend, neighbours, convolve))

        @block.scalar
        def _(act):
            act.wait_ge(done["u_ps"], 1)
            act.copy(u[:, :, :], pB[0:C, 0:HEADS * C].rearrange("c (h o) -> c h o", h=HEADS)).then_inc(done["u_ready"], 1)
            act.wait_ge(done["loaded_weights"], 16 * 8)

            def attend(b, p):
                yield A(9)
                act.wait_ge(done["k_max"], b + 1)
                act.wait_ge(*since("ek_T", b))
                act.wait_ge(*since("k_rec", b))
                act.activation(ek[:, :], pA[:, :], ACT.Exp, bias=kstat[:, 0:1], scale=1.0,
                               accum_out=kstat[:, 1:2]).then_inc(done["k_exp"], 1)
                act.wait_ge(done["yT_ps"], b + 1)
                act.wait_ge(*since("ky_ps", b))
                act.copy(yT[:, :, :], pB[:, :].rearrange("p (j q) -> p j q", j=NJ)).then_inc(done["yT_copied"], 1)
                yield A(11)
                act.wait_ge(done["ek_T"], b + 1)
                act.copy(ekT[:, :, :], pA[:, :].rearrange("p (t q) -> p t q", t=NT)).then_inc(done["ekT_copied"], 1)
                yield A(13)
                act.wait_ge(done["ky_ps"], b + 1)
                act.wait_ge(*since("m_ps", b))
                act.copy(kyT[:, :], pB[0:C, 0:P]).then_inc(done["ky_copied"], 1)
                yield A(14)
                act.wait_ge(done["q_sub"], b + 1)
                act.wait_ge(*since("q_norm", b))
                act.activation(qe[:, :, :], qs[:, :, :], ACT.Exp).then_inc(done["q_exp"], 1)
                yield A(18)
                act.wait_ge(done["q_T"], b + 1)
                act.wait_ge(*since("att_ps", b))
                act.copy(qh[:, :], pA[:, :]).then_inc(done["qh_copied"], 1)
                yield A(20)
                act.wait_ge(done["att_ps"], b + 1)
                act.wait_ge(*since("att_normed", b))
                act.wait_ge(*since("att_stat", b))
                act.activation(att[:, :], pB[:, :], ACT.Identity, bias=vector("b_out")).then_inc(done["att_copied"], 1)
                yield A(28)
                act.wait_ge(done["att_bias"], b + 1)
                act.wait_ge(*since("x1_ready", b))
                act.activation(attn[:, :], att[:, :], ACT.Identity, bias=st["att"][:, 15:16],
                               scale=st["att"][:, 14:15]).then_inc(done["att_normed"], 1)
                yield A(37)
                act.wait_ge(done["y1_ready"], b + 1)
                act.wait_ge(*since("ss_ps", b))
                act.activation(sq[:, :], y1[:, :], ACT.Square).then_inc(done["sq_ready"], 1)
                yield A(45)
                act.wait_ge(done["xn_ready"], b + 1)
                act.wait_ge(*since(f"stacked{1 - p}", 16 * 6 * (b + p)))
                act.copy(xhi[:, :], xn[p][:, :]).then_inc(done["hi_ready"], 1)

            def neighbours(b, p):
                yield 0.0
                act.wait_ge(done["xt1_ps"], b + 1)
                act.wait_ge(*since("g1_ps", b - 1))
                act.copy(xt1[p][:, :, :, :], pB[:, :].rearrange("p (j h c) -> p j h c", j=NJ, h=2)).then_inc(done["xt1_copied"], 1)
                for r in range(NT):
                    yield r + 0.01
                    act.wait_ge(done["tile_sim_ps"], NT * b + r + 1)
                    act.wait_ge(*since("tile_adj", NT * b + r - 1))
                    act.copy(sim[r % 2][:, :], pS[:, :]).then_inc(done["tile_sim"], 1)
                    if r >= 2:
                        yield r - 2 + LATE_T + 0.05
                        copy_transposed(b, p, r - 2)

            def copy_transposed(b, p, r):
                if r == 0:
                    act.wait_ge(*since("g2_ps", b - 1))
                act.wait_ge(done["tile_T"], NT * b + r + 1)
                act.copy(adjT[p][:, :, r * P:(r + 1) * P], pT[:, :, :]).then_inc(done["tile_adjT"], 1)

            def silu_parts(b, tag, src, half, tanh):
                act.wait_ge(done[f"{tag}_bias"], b + 1)
                act.wait_ge(*since({"g1": "y2_ready", "g2": "y3_ready"}[tag], b))
                act.activation(half[:, :], src[:, :], ACT.Identity, bias=st[tag][:, 15:16],
                               scale=st[tag][:, 14:15]).then_inc(done[f"{tag}_half"], 1)
                act.activation(tanh[:, :], src[:, :], ACT.Tanh, bias=st[tag][:, 15:16],
                               scale=st[tag][:, 14:15]).then_inc(done[f"{tag}_tanh"], 1)

            def convolve(b, p):
                for r in (NT - 2, NT - 1):
                    yield 0.04 + 0.09 * (r - NT + 2)
                    copy_transposed(b, p, r)
                yield V(3)
                act.wait_ge(done["v_spread"], b + 1)
                act.wait_ge(*since("g2_copied", b))
                act.copy(vbc[:, :], pC[:, :]).then_inc(done["v_bc"], 1)
                yield V(18)
                silu_parts(b, "g1", g, zh, th)
                yield V(19.5)
                act.wait_ge(done["xt2_ps"], b + 1)
                act.wait_ge(*since("g2_ps", b))
                act.copy(xt2[:, :, :, :], pC[:, :].rearrange("p (j h c) -> p j h c", j=NJ, h=2)).then_inc(done["xt2_copied"], 1)
                yield V(33)
                silu_parts(b, "g2", g2, zh2, th2)

            samples(act, (attend, neighbours, convolve))

        @block.vector
        def _(dve):
            dve.wait_ge(done["loaded_weights"], 16 * 8)
            dve.wait_ge(done["prepared"], 3)
            dve.tensor_scalar(mark16[:, :], ident, MARK, None, ALU.mult).then_inc(done["prepared"], 1)
            dve.tensor_copy(ident16[:, :], ident).then_inc(done["prepared"], 1)
            for h in range(2):
                c = slice(h * C, (h + 1) * C)
                dve.tensor_scalar(w1[c, c], w1r[c, :], 1.0 / XSCALE, None, ALU.mult).then_inc(done["prepared"], 1)
                dve.tensor_copy(w2[c, c], w2r[c, :]).then_inc(done["prepared"], 1)

            def stats(b, tag, src, ready, shift=None):
                dve.wait_ge(done[ready], b + 1)
                dve.wait_ge(*since(f"{tag}_aggr", b))
                dve.bn_stats(st[tag][:, 0:6], src).then_inc(done[f"{tag}_stat"], 1)
                constant_first(dve, b + 1, b, b)
                dve.wait_ge(done[f"{tag}_stat"], b + 1)
                dve.wait_ge(*since(f"{tag}_mean_ps", b))
                dve.wait_ge(*since(f"{tag}_sq", b))
                dve.bn_aggr(st[tag][:, 6:8], st[tag][:, 0:6]).then_inc(done[f"{tag}_aggr"], 1)
                if shift is not None:
                    dve.wait_ge(done[f"{tag}_aggr"], b + 1)
                    dve.tensor_tensor(st[tag][:, 6:7], st[tag][:, 6:7], shift, ALU.add).then_inc(done[f"{tag}_mean"], 1)

            def deviation(b, tag, ps):
                dve.wait_ge(done[f"{tag}_mean_ps"], b + 1)
                dve.tensor_scalar(st[tag][:, 8:9], ps[:, 0:1], -1.0, None, ALU.mult)
                dve.tensor_tensor(st[tag][:, 9:10], st[tag][:, 6:7], ps[:, 0:1], ALU.subtract).then_inc(done[f"{tag}_dev"], 1)
                dve.wait_ge(done[f"{tag}_dev"], b + 1)
                dve.wait_ge(*since(f"{tag}_var_ps", b))
                dve.scalar_tensor_tensor(out=st[tag][:, 10:11], in0=st[tag][:, 9:10], scalar=st[tag][:, 9:10],
                                         in1=st[tag][:, 7:8], op0=ALU.mult, op1=ALU.add).then_inc(done[f"{tag}_sq"], 1)

            def variance(b, tag, ps):
                dve.wait_ge(done[f"{tag}_var_ps"], b + 1)
                dve.wait_ge(*since(f"{tag}_rstd", b))
                dve.tensor_scalar(st[tag][:, 12:13], ps[:, 1:2], EPS, None, ALU.add).then_inc(done[f"{tag}_veps"], 1)

            def affine(b, tag, weight, bias, half, shift=None):
                f = 0.5 if half else 1.0
                t = st[tag]
                dve.wait_ge(done[f"{tag}_rstd"], b + 1)
                dve.wait_ge(*since({"att": "att_normed", "g1": "g1_tanh", "g2": "g2_tanh"}[tag], b))
                dve.tensor_scalar(t[:, 14:15], t[:, 13:14], weight, f, ALU.mult, ALU.mult).then_inc(done[f"{tag}_scale"], 1)
                if shift is not None:
                    dve.tensor_tensor(t[:, 16:17], t[:, 8:9], shift, ALU.add)
                else:
                    dve.tensor_copy(t[:, 16:17], t[:, 8:9])
                dve.tensor_scalar(t[:, 17:18], bias, f, None, ALU.mult).then_inc(done[f"{tag}_scale"], 1)
                dve.wait_ge(done[f"{tag}_scale"], 2 * (b + 1))
                dve.scalar_tensor_tensor(out=t[:, 15:16], in0=t[:, 16:17], scalar=t[:, 14:15], in1=t[:, 17:18],
                                         op0=ALU.mult, op1=ALU.add).then_inc(done[f"{tag}_bias"], 1)

            def attend(b, p):
                yield A(0)
                dve.wait_ge(done[f"x_in{p}"], 16 * (b - p + 2))
                dve.wait_ge(*since("in_aggr", b))
                dve.bn_stats(st["in"][:, 0:6], xin[p][:, :]).then_inc(done["in_stat"], 1)
                constant_first(dve, b + 1, b, b)
                dve.wait_ge(done["in_stat"], b + 1)
                dve.wait_ge(*since("in_mean_ps", b))
                dve.wait_ge(*since("in_sq", b))
                dve.bn_aggr(st["in"][:, 6:8], st["in"][:, 0:6]).then_inc(done["in_aggr"], 1)
                yield A(2)
                deviation(b, "in", pB)
                yield A(4)
                variance(b, "in", pB)
                yield A(6)
                dve.wait_ge(done["in_rstd"], b + 1)
                dve.wait_ge(*since("q_ps", b))
                dve.tensor_scalar(y[:, :], xin[p][:, :], st["in"][:, 8:9], st["in"][:, 13:14], ALU.add,
                                  ALU.mult).then_inc(done["y_ready"], 1)
                yield A(8)
                dve.wait_ge(done["k_ps"], b + 1)
                dve.tensor_reduce(kstat[:, 0:1], pA[:, :], AX.X, ALU.max, negate=True).then_inc(done["k_max"], 1)
                yield A(10)
                dve.wait_ge(done["k_exp"], b + 1)
                dve.reciprocal(kstat[:, 2:3], kstat[:, 1:2]).then_inc(done["k_rec"], 1)
                yield A(13)
                dve.wait_ge(done["q_ps"], b + 1)
                q_ps = pA[:, :].rearrange("p (g d) -> p g d", d=D)
                dve.tensor_reduce(qmax[:, :], q_ps, AX.X, ALU.max).then_inc(done["q_max"], 1)
                dve.wait_ge(done["q_max"], b + 1)
                dve.wait_ge(*since("q_exp", b))
                dve.tensor_tensor(qs[:, :, :], q_ps, qmax[:, :].unsqueeze(2).broadcast_to([P, NT * HEADS, D]),
                                  ALU.subtract).then_inc(done["q_sub"], 1)
                yield A(15)
                dve.wait_ge(done["m_ps"], b + 1)
                dve.wait_ge(done["k_rec"], b + 1)
                dve.wait_ge(*since("att_ps", b))
                dve.tensor_scalar(mT[:, :], pB[:, 256:256 + C], kstat[:, 2:3], SCALE, ALU.mult, ALU.mult).then_inc(done["m_copied"], 1)
                yield A(15.5)
                dve.wait_ge(done["q_exp"], b + 1)
                dve.tensor_reduce(qsum[:, :], qe[:, :, :], AX.X, ALU.add).then_inc(done["q_sum"], 1)
                dve.wait_ge(done["q_sum"], b + 1)
                dve.wait_ge(*since("q_norm", b))
                dve.reciprocal(qrec[:, :], qsum[:, :]).then_inc(done["q_rec"], 1)
                yield A(21)
                stats(b, "att", att[:, :], "att_copied")
                yield A(23)
                deviation(b, "att", pB)
                yield A(25)
                variance(b, "att", pB)
                yield A(27)
                affine(b, "att", vector("gn_weight"), vector("gn_bias"), False)
                yield A(30)
                stats(b, "mid", x1[:, :], "x1_ready")
                yield A(32)
                deviation(b, "mid", pB)
                yield A(34)
                variance(b, "mid", pB)
                yield A(36)
                dve.wait_ge(done["mid_rstd"], b + 1)
                dve.wait_ge(*since("xn_ready", b))
                dve.wait_ge(*since("sq_ready", b))
                dve.tensor_scalar(y1[:, :], x1[:, :], st["mid"][:, 8:9], st["mid"][:, 13:14], ALU.add,
                                  ALU.mult).then_inc(done["y1_ready"], 1)
                yield A(39)
                dve.wait_ge(done["ss_ps"], b + 1)
                dve.wait_ge(*since("rn_ready", b))
                dve.wait_ge(*since("sn_ready", b))
                dve.tensor_copy(ss[:, :], pB[:, 0:NT])
                dve.tensor_scalar(ssq[:, :], pB[:, 0:NT], 1e-24, 1.0 / SSCALE, ALU.max, ALU.mult).then_inc(done["ss_copied"], 1)
                yield A(42)
                dve.wait_ge(done["rn_ready"], b + 1)
                dve.wait_ge(done["ss_copied"], b + 1)
                dve.tensor_tensor(sn[:, :], ss[:, :], rn[:, :], ALU.mult).then_inc(done["sn_ready"], 1)
                dve.wait_ge(done["sn_ready"], b + 1)
                dve.wait_ge(*since("v_tot", b - 1))
                dve.tensor_tensor(selfsim[p][:, :], sn[:, :], rn[:, :], ALU.mult).then_inc(done["selfsim_ready"], 1)
                dve.wait_ge(done["rn_T"], b + 1)
                dve.wait_ge(*since("rn_spread", b))
                dve.tensor_copy(rnT[:, :], pB[0:NT, P:2 * P]).then_inc(done["rnT_copied"], 1)
                yield A(44)
                dve.wait_ge(done["rn_spread"], b + 1)
                dve.wait_ge(*since("xt1_ps", b - 1))
                dve.wait_ge(*since("hi_ready", b - 1))
                dve.tensor_tensor(xn[p][:, :], y1[:, :], pB[:, :], ALU.mult).then_inc(done["xn_ready"], 1)
                yield A(46)
                dve.wait_ge(done["hi_ready"], b + 1)
                dve.wait_ge(done["xn_ready"], b + 1)
                dve.wait_ge(*since(f"stacked{1 - p}", 16 * 6 * (b + p)))
                dve.tensor_tensor(xlo[:, :], xn[p][:, :], xhi[:, :], ALU.subtract).then_inc(done["lo_ready"], 1)

            def neighbours(b, p):
                for r in range(NT):
                    n = NT * b + r
                    yield r + 0.2
                    constant_first(dve, n + 1, b)
                    dve.wait_ge(done["tile_sim"], n + 1)
                    dve.wait_ge(*since("v_sum", b))
                    dve.max(top[:, r, :], sim[r % 2][:, :]).then_inc(done["tile_top"], 1)
                    yield r + 0.35
                    constant_first(dve, n + 1, n - 1)
                    dve.wait_ge(done["tile_top"], n + 1)
                    dve.wait_ge(*since("tile_adj", n - 1))
                    dve.match_replace(out=rest[r % 2][:, :], in_to_replace=top[:, r, :], in_values=sim[r % 2][:, :],
                                      imm_value=0.0).then_inc(done["tile_rest"], 1)
                yield 7.45
                dve.tensor_reduce(vsum[:, :], top[:, :, :], AX.X, ALU.add).then_inc(done["v_sum"], 1)
                dve.wait_ge(done["v_sum"], b + 1)
                dve.wait_ge(done["selfsim_ready"], b + 1)
                dve.scalar_tensor_tensor(out=vtot[:, :], in0=vsum[:, :], scalar=1e-6 * SSCALE, in1=selfsim[p][:, :],
                                         op0=ALU.add, op1=ALU.add).then_inc(done["v_tot"], 1)
                dve.wait_ge(done["v_tot"], b + 1)
                dve.wait_ge(*since("v_T", b - 1))
                dve.reciprocal(vrec[p][:, :], vtot[:, :]).then_inc(done["v_rec"], 1)

            def gcn(b, tag, first, dst, tanh, half, act_out, act_name, bias, gamma, beta):
                yield V(first)
                dve.wait_ge(done[f"{tag}_ps"], b + 1)
                dve.wait_ge(done["v_bc"], b + 1)
                dve.wait_ge(*since(f"{tag}_tanh", b))
                dve.wait_ge(*since(f"{tag}_stat", b))
                dve.tensor_tensor(dst[:, :], pC[:, :], vbc[:, :], ALU.mult).then_inc(done[f"{tag}_copied"], 1)
                stats(b, tag, dst[:, :], f"{tag}_copied", shift=vector(bias))
                yield V(first + 2)
                deviation(b, tag, pC)
                yield V(first + 4)
                variance(b, tag, pC)
                yield V(first + 5.5)
                affine(b, tag, vector(gamma), vector(beta), True, shift=vector(bias))
                yield V(first + 7)
                dve.wait_ge(done[f"{tag}_tanh"], b + 1)
                if tag == "g1":
                    dve.wait_ge(*since("xt2_ps", b))
                else:
                    dve.wait_ge(*since("res_ready", b))
                dve.scalar_tensor_tensor(out=act_out[:, :], in0=tanh[:, :], scalar=1.0, in1=half[:, :], op0=ALU.add,
                                         op1=ALU.mult).then_inc(done[act_name], 1)

            def convolve(b, p):
                yield V(1)
                dve.wait_ge(done["v_T"], b + 1)
                dve.wait_ge(*since("v_spread", b))
                dve.tensor_copy(vrT[:, :], pC[0:NT, 0:P]).then_inc(done["vT_copied"], 1)
                yield from gcn(b, "g1", 12, g, th, zh, y2, "y2_ready", "b1", "gamma1", "beta1")
                yield from gcn(b, "g2", 28, g2, th2, zh2, y3, "y3_ready", "b2", "gamma2", "beta2")

            samples(dve, (attend, neighbours, convolve))

        @block.tensor
        def _(pe):
            pe.wait_ge(done["loaded_weights"], 16 * 8)
            pe.wait_ge(done["prepared"], PREPARED)
            for h in range(HEADS):
                mm = pe.matmul(pB[0:C, h * C:(h + 1) * C], wv[:, h, :], wo[:, h, :], start=True, stop=True)
            mm.then_inc(done["u_ps"], 1)
            pe.wait_ge(done["u_ready"], 1)

            def average(b, tag, ps, avg, mean_ready):
                pe.wait_ge(done[mean_ready], b + 1)
                pe.matmul(ps[:, 0:1], const(avg), st[tag][:, 6:7], start=True, stop=True).then_inc(done[f"{tag}_mean_ps"], 1)

            def average_sq(b, tag, ps, avg):
                pe.wait_ge(done[f"{tag}_sq"], b + 1)
                pe.matmul(ps[:, 1:2], const(avg), st[tag][:, 10:11], start=True, stop=True).then_inc(done[f"{tag}_var_ps"], 1)

            def token_block(t):
                h, j = divmod(t, NJ)
                return slice(h * C, (h + 1) * C), slice(j * P, (j + 1) * P)

            def attend(b, p):
                yield A(1)
                pe.wait_ge(*since("xt1_copied", b))
                average(b, "in", pB, "avg_pair", "in_aggr")
                yield A(3)
                average_sq(b, "in", pB, "avg_pair")
                yield A(7)
                pe.wait_ge(done["y_ready"], b + 1)
                pe.wait_ge(*since("qh_copied", b))
                for h in range(2):
                    c = slice(h * C, (h + 1) * C)
                    mm = pe.matmul(pA[:, h * H:(h + 1) * H], wk[c, :], y[c, :], start=True, stop=True)
                mm.then_inc(done["k_ps"], 1)
                pe.wait_ge(done["in_veps"], b + 1)
                for j in range(NJ):
                    mm = pe.transpose(pB[:, j * P:(j + 1) * P], y[:, j * P:(j + 1) * P], ident)
                mm.then_inc(done["yT_ps"], 1)
                yield A(10)
                pe.wait_ge(done["k_exp"], b + 1)
                for t in range(NT):
                    mm = pe.transpose(pA[:, t * P:(t + 1) * P], ek[:, t * P:(t + 1) * P], ident)
                mm.then_inc(done["ek_T"], 1)
                yield A(12)
                pe.wait_ge(done["ekT_copied"], b + 1)
                for t in range(NT):
                    c, tok = token_block(t)
                    mm = pe.matmul(pA[:, t * P:(t + 1) * P], y[c, tok], wq[c, :], start=True, stop=True)
                mm.then_inc(done["q_ps"], 1)
                pe.wait_ge(done["yT_copied"], b + 1)
                for t in range(NT):
                    h, j = divmod(t, NJ)
                    mm = pe.matmul(pB[0:C, 0:P], yT[:, j, h * C:(h + 1) * C], ekT[:, t, :], start=(t == 0), stop=(t == NT - 1))
                mm.then_inc(done["ky_ps"], 1)
                yield A(14)
                constant_first(pe, b + 1)
                pe.wait_ge(done["ky_copied"], b + 1)
                for h in range(HEADS):
                    mm = pe.matmul(pB[h * D:(h + 1) * D, 256:256 + C], kyT[:, h * D:(h + 1) * D], u[:, h, :], start=True, stop=True)
                mm.then_inc(done["m_ps"], 1)
                yield A(17)
                pe.wait_ge(done["q_norm"], b + 1)
                for t in range(NT):
                    mm = pe.transpose(pA[:, t * P:(t + 1) * P], qn[:, t * HEADS:(t + 1) * HEADS, :], ident)
                mm.then_inc(done["q_T"], 1)
                yield A(19)
                pe.wait_ge(done["qh_copied"], b + 1)
                pe.wait_ge(done["m_copied"], b + 1)
                for h in range(2):
                    mm = pe.matmul(pB[h * C:(h + 1) * C, :], mT[:, :], qh[:, h * H:(h + 1) * H], start=True, stop=True)
                mm.then_inc(done["att_ps"], 1)
                yield A(22)
                pe.wait_ge(done["att_copied"], b + 1)
                average(b, "att", pB, "avg_sample", "att_aggr")
                yield A(24)
                average_sq(b, "att", pB, "avg_sample")
                yield A(31)
                pe.wait_ge(done["att_veps"], b + 1)
                average(b, "mid", pB, "avg_pair", "mid_aggr")
                yield A(33)
                average_sq(b, "mid", pB, "avg_pair")
                yield A(38)
                pe.wait_ge(done["sq_ready"], b + 1)
                pe.wait_ge(done["mid_veps"], b + 1)
                for j in range(NJ):
                    mm = pe.matmul(pB[:, j:j + NJ + 1:NJ], sq[:, j * P:(j + 1) * P], const("halves"), start=True, stop=True)
                mm.then_inc(done["ss_ps"], 1)
                yield A(41)
                pe.wait_ge(done["rn_ready"], b + 1)
                pe.transpose(pB[0:NT, P:2 * P], rn[:, :], ident).then_inc(done["rn_T"], 1)
                yield A(43)
                pe.wait_ge(done["rnT_copied"], b + 1)
                for j in range(NJ):
                    mm = pe.matmul(pB[:, j * P:(j + 1) * P], spread[0:NT, j, :], rnT[:, :], start=True, stop=True)
                mm.then_inc(done["rn_spread"], 1)

            def neighbours(b, p):
                yield -0.02
                pe.wait_ge(done["xn_ready"], b + 1)
                for j in range(NJ):
                    mm = pe.matmul(pB[:, j * P:(j + 1) * P], xn[p][:, j * P:(j + 1) * P], w1[:, :], start=True, stop=True)
                mm.then_inc(done["xt1_ps"], 1)
                pe.wait_ge(done[f"stacked{p}"], 16 * 6 * (b - p + 2))
                for r in range(NT):
                    yield r + (0.0 if r else -0.01)
                    pe.wait_ge(*since("tile_sim", NT * b + r))
                    rows = slice(r * P, (r + 1) * P)
                    for h in range(2):
                        tok = slice(h * H, (h + 1) * H)
                        pe.matmul(pS[:, tok], hilo[p][:, rows], hihi[p][:, tok], start=True, stop=False)
                        if r // NJ == h:
                            pe.matmul(pS[:, rows], ident16[:, :], mark16[:, :], start=False, stop=False,
                                      skip_group_check=True)
                        mm = pe.matmul(pS[:, tok], hilo[p][:, rows], lolo[p][:, tok], start=False, stop=True)
                    mm.then_inc(done["tile_sim_ps"], 1)
                    if r >= 2:
                        yield r - 2 + LATE_T
                        transpose_tile(b, r - 2)

            def transpose_tile(b, r):
                n = NT * b + r
                pe.wait_ge(done["tile_adj"], n + 1)
                pe.wait_ge(*since("tile_adjT", n))
                for t in range(NT):
                    mm = pe.transpose(pT[:, t, :], adj[r % 2][:, t * P:(t + 1) * P], ident)
                mm.then_inc(done["tile_T"], 1)

            def aggregate(xt, p, first, signal):
                for t in range(NT):
                    yield V(first + t)
                    for h in range(2):
                        mm = pe.matmul(pC[h * C:(h + 1) * C, :], xt[:, t % NJ, t // NJ, :], adjT[p][:, t, h * H:(h + 1) * H],
                                       start=(t == 0), stop=(t == NT - 1))
                mm.then_inc(done[signal], 1)

            def convolve(b, p):
                for r in (NT - 2, NT - 1):
                    yield 0.03 + 0.09 * (r - NT + 2)
                    transpose_tile(b, r)
                yield V(0)
                pe.wait_ge(done["v_rec"], b + 1)
                pe.wait_ge(*since("g2_veps", b))
                pe.transpose(pC[0:NT, 0:P], vrec[p][:, :], ident).then_inc(done["v_T"], 1)
                yield V(2)
                pe.wait_ge(done["vT_copied"], b + 1)
                for j in range(NJ):
                    mm = pe.matmul(pC[:, j * P:(j + 1) * P], spread[0:NT, j, :], vrT[:, :], start=True, stop=True)
                mm.then_inc(done["v_spread"], 1)
                yield V(3.5)
                pe.wait_ge(done["v_bc"], b + 1)
                pe.wait_ge(done["xt1_copied"], b + 1)
                pe.wait_ge(done["tile_adjT"], NT * (b + 1))
                yield from aggregate(xt1[p], p, 4, "g1_ps")
                yield V(13)
                pe.wait_ge(done["g1_copied"], b + 1)
                average(b, "g1", pC, "avg_group", "g1_mean")
                yield V(15)
                average_sq(b, "g1", pC, "avg_group")
                yield V(19.3)
                pe.wait_ge(done["y2_ready"], b + 1)
                pe.wait_ge(done["g1_veps"], b + 1)
                for j in range(NJ):
                    mm = pe.matmul(pC[:, j * P:(j + 1) * P], y2[:, j * P:(j + 1) * P], w2[:, :], start=True, stop=True)
                mm.then_inc(done["xt2_ps"], 1)
                yield V(19.8)
                pe.wait_ge(done["xt2_copied"], b + 1)
                yield from aggregate(xt2, p, 20, "g2_ps")
                yield V(29)
                pe.wait_ge(done["g2_copied"], b + 1)
                average(b, "g2", pC, "avg_group", "g2_mean")
                yield V(31)
                average_sq(b, "g2", pC, "avg_group")

            samples(pe, (attend, neighbours, convolve))


def kernel(**inputs):
    import concourse.bacc as bacc
    from concourse.bass_utils import run_bass_kernel_spmd as run

    a = {n: np.asarray(v) for n, v in inputs.items()}
    x = a["x"]
    B, C, Hh, Ww = x.shape
    w_qkv = a["L0_conv_w_qkv"]
    hid = w_qkv.shape[0] // 3

    def twice(m):
        return np.ascontiguousarray(np.concatenate([m, m], axis=0))

    cols = [a["L0_conv_b_out"], a["L0_conv_gn_weight"], a["L0_conv_gn_bias"], a["L1_conv_b1"], a["L1_conv_gamma1"],
            a["L1_conv_beta1"], a["L1_conv_b2"], a["L1_conv_gamma2"], a["L1_conv_beta2"]]
    arrays = {
        "x": np.ascontiguousarray(x.reshape(B, C, Hh * Ww)),
        "w_q": twice(w_qkv[0:hid].T),
        "w_k": twice(w_qkv[hid:2 * hid].T),
        "w_v": np.ascontiguousarray(w_qkv[2 * hid:].reshape(HEADS, -1, C).transpose(1, 0, 2)),
        "w_o": np.ascontiguousarray(a["L0_conv_w_out"].T.reshape(HEADS, -1, C).transpose(1, 0, 2)),
        "w_1": twice(a["L1_conv_w1"]),
        "w_2": twice(a["L1_conv_w2"]),
        "vectors": twice(np.stack(cols, axis=1)),
        "constants": shape_constants(C),
    }
    nc = bacc.Bacc("TRN2", target_bir_lowering=False, num_devices=1)
    args = [nc.dram_tensor(n, v.shape, mybir.dt.from_np(v.dtype), kind="ExternalInput").ap() for n, v in arrays.items()]
    out = nc.dram_tensor("out", (B, C, Hh * Ww), F32, kind="ExternalOutput").ap()
    build(nc, *args, out)
    r = run(nc, [arrays], core_ids=[0])
    return r.results[0]["out"].reshape(B, C, Hh, Ww)
```

```python
from contextlib import ExitStack

import numpy as np

import concourse.bass as bass
from concourse import mybir

ALU = mybir.AluOpType
ACT = mybir.ActivationFunctionType
AX = mybir.AxisListType
F32 = mybir.dt.float32
F16 = mybir.dt.float16

P = 128
HEADS = 4
TOP = 8
XSCALE = 64.0
SSCALE = XSCALE * XSCALE
MARK = -2.5 * SSCALE
EPS = 1e-5

CONST_PARTS = [("ident", P), ("avg_pair", P), ("avg_sample", P), ("avg_group", P), ("halves", 2)]
VECTORS = ["b_out", "gn_weight", "gn_bias", "b1", "gamma1", "beta1", "b2", "gamma2", "beta2"]


TIMES = {
    "sync": {
        "neighbours": [599],
        "convolve": [500, 596, 774],
        "unit": [601, 602, 667, 668],
        "attend": [583, 597],
    },
    "gpsimd": {
        "neighbours": [308, 376, 385, 542, 559, 560, 585, 712],
        "convolve": [416, 682, 731],
        "unit": [235, 236, 309, 526],
        "attend": [1, 562],
    },
    "scalar": {
        "neighbours": [28, 226, 282, 306, 474, 531, 618, 664, 775],
        "transposes": [399, 441, 490, 535, 597, 632, 673, 704, 766, 776, 793, 794],
        "convolve": [27, 225, 252, 260, 579, 586, 630, 800, 801],
        "unit": [261, 410, 739],
        "attend": [364, 434, 483, 635, 669, 786, 802],
    },
    "vector": {
        "neighbours": [211, 214, 268, 364, 394, 530, 579, 629, 666, 703, 718, 734, 742, 754, 792, 800, 801],
        "convolve": [192, 535, 558, 568, 572, 624, 691, 766, 767, 775, 788, 793, 802],
        "unit": [33, 65, 164, 181, 246, 308, 367, 403, 570, 689, 690, 733, 753, 768],
        "attend": [3, 63, 143, 166, 276, 404, 706, 732, 738, 740, 743],
    },
    "tensor": {
        "neighbours": [8, 9, 132, 216, 403, 473, 532, 602, 752],
        "transposes": [277, 374, 452, 498, 538, 554, 663, 697, 743, 779, 797, 801],
        "convolve": [0, 40, 94, 134, 137, 162, 163, 164, 165, 251, 252, 367, 368, 371, 455, 486, 559, 625, 627, 646, 677,
                    687, 698, 731, 732, 733, 789, 800],
        "unit": [57, 122, 248, 358, 451, 535],
        "attend": [44, 60, 146, 366, 436, 496, 553, 676, 788, 802],
    },
}


def column_of(parts, name):
    at = 0
    for n, width in parts:
        if n == name:
            return at, at + width
        at += width


def shape_constants(C):
    p = np.arange(P)
    channel = p % C
    out = {"ident": np.eye(P)}
    for name, size in (("avg_pair", 2), ("avg_sample", C), ("avg_group", C // 4)):
        same = channel[:, None] // size == channel[None, :] // size
        out[name] = same / same.sum(1, keepdims=True)
    out["halves"] = np.arange(P)[:, None] // C == np.arange(2)[None, :]
    return np.concatenate([out[n] for n, _ in CONST_PARTS], axis=1).astype(np.float32)


def build(nc, x, w_q, w_k, w_v, w_o, w_1, w_2, vectors, constants, out):
    B, C, N = x.shape
    H = N // 2
    NT = N // P
    NJ = H // P
    D = P // HEADS
    SCALE = float(D) ** -0.5
    assert C == 64 and 2 * C == P and H == 512

    ctx = ExitStack()
    with ctx:
        def sb(name, shape, dt=F32):
            return ctx.enter_context(nc.sbuf_tensor(name, shape, dt))

        def sem(name):
            return ctx.enter_context(nc.semaphore(name))

        cst = sb("cst", [P, constants.shape[1]])
        vec = sb("vec", [P, vectors.shape[1]])
        wq = sb("wq", [P, P])
        wk = sb("wk", [P, P])
        wv = sb("wv", [D, HEADS, C])
        wo = sb("wo", [D, HEADS, C])
        w1r = sb("w1r", [P, C])
        w2r = sb("w2r", [P, C])
        w1 = sb("w1", [P, P])
        w2 = sb("w2", [P, P])
        u = sb("u", [P, HEADS, C])
        ident16 = sb("ident16", [P, P], F16)
        mark16 = sb("mark16", [P, P], F16)
        minus_half = sb("minus_half", [P, NT])

        def const(name):
            a, b = column_of(CONST_PARTS, name)
            return cst[:, a:b]

        def vector(name):
            i = VECTORS.index(name)
            return vec[:, i:i + 1]

        ident = const("ident")

        xa = [sb(f"xa{i}", [P, H]) for i in range(2)]
        y = sb("y", [P, H])
        ek = sb("ek", [P, N])
        ekT = sb("ekT", [P, NT, P])
        yT = sb("yT", [P, NJ, P])
        kyT = sb("kyT", [P, P])
        mT = sb("mT", [P, C])
        qs = sb("qs", [P, NT * HEADS, D])
        qe = sb("qe", [P, NT * HEADS, D])
        qn = sb("qn", [P, NT * HEADS, D])
        qh = sb("qh", [P, N])
        att = sb("att", [P, H])

        xu = [sb(f"xu{i}", [P, H]) for i in range(2)]
        attn = sb("attn", [P, H])
        x1 = sb("x1", [P, H])
        y1 = sb("y1", [P, H])
        sq = sb("sq", [P, H])
        xn = [sb(f"xn{i}", [P, H]) for i in range(2)]
        xhi = sb("xhi", [P, H], F16)
        xlo = sb("xlo", [P, H], F16)
        hilo = [sb(f"hilo{i}", [P, N], F16) for i in range(2)]
        hihi = [sb(f"hihi{i}", [P, N], F16) for i in range(2)]
        lolo = [sb(f"lolo{i}", [P, N], F16) for i in range(2)]
        st = {n: sb(f"st_{n}", [P, 24]) for n in ("in", "att", "mid", "g1", "g2")}
        kstat = sb("kstat", [P, 4])
        qmax = sb("qmax", [P, NT * HEADS])
        qsum = sb("qsum", [P, NT * HEADS])
        qrec = sb("qrec", [P, NT * HEADS])
        ss = sb("ss", [P, NT])
        ssq = sb("ssq", [P, NT])
        rn = sb("rn", [P, NT])
        sn = sb("sn", [P, NT])
        selfsim = [sb(f"selfsim{i}", [P, NT]) for i in range(2)]
        rnT = sb("rnT", [NT, P])
        rbc = sb("rbc", [P, H])

        x1c = [sb(f"x1c{i}", [P, H]) for i in range(2)]
        xt1 = [sb(f"xt1_{i}", [P, NJ, 2, C]) for i in range(2)]
        sim = [sb(f"sim{i}", [P, N]) for i in range(4)]
        rest = [sb(f"rest{i}", [P, N]) for i in range(2)]
        adj = [sb(f"adj{i}", [P, N]) for i in range(2)]
        top = sb("top", [P, NT, TOP])
        adjT = [sb(f"adjT{i}", [P, NT, N]) for i in range(2)]
        vsum = sb("vsum", [P, NT])
        vtot = sb("vtot", [P, NT])
        vrec = [sb(f"vrec{i}", [P, NT]) for i in range(2)]

        vrT = sb("vrT", [NT, P])
        vbc = sb("vbc", [P, H])
        g = sb("g", [P, H])
        zh = sb("zh", [P, H])
        th = sb("th", [P, H])
        y2 = sb("y2", [P, H])
        xt2 = sb("xt2", [P, NJ, 2, C])
        g2 = sb("g2", [P, H])
        zh2 = sb("zh2", [P, H])
        th2 = sb("th2", [P, H])
        y3 = sb("y3", [P, H])
        res = [sb(f"res{i}", [P, H]) for i in range(2)]

        x1_kept = nc.dram_tensor("x1_kept", (B, P, H), F32, kind="Internal").ap()
        rn_row = nc.dram_tensor("rn_row", (B, NT, P), F32, kind="Internal").ap()
        v_row = nc.dram_tensor("v_row", (B, NT, P), F32, kind="Internal").ap()

        pS = ctx.enter_context(nc.psum_tensor("pS", [P, N], F32))
        pT = ctx.enter_context(nc.psum_tensor("pT", [P, NJ, P], F32))
        pA = ctx.enter_context(nc.psum_tensor("pA", [P, N], F32))
        pB = ctx.enter_context(nc.psum_tensor("pB", [P, H], F32))
        pD = ctx.enter_context(nc.psum_tensor("pD", [P, H], F32))
        pC = ctx.enter_context(nc.psum_tensor("pC", [P, H], F32))

        names = """loaded_weights prepared u_ps u_ready
            xa_in0 xa_in1 xu_in0 xu_in1 x1_back0 x1_back1 in_shift mid_shift in_stat in_aggr in_mean_ps in_dev in_sq in_var_ps in_veps in_rstd y_ready
            k_ps k_max k_exp ek_T ekT_copied yT_ps yT_copied ky_ps ky_copied k_rec m_ps m_copied
            q_ps q_max q_sub q_exp q_sum q_rec q_norm q_T qh_copied att_ps att_copied
            att_stat att_aggr att_mean_ps att_dev att_sq att_var_ps att_veps att_rstd att_scale att_bias
            att_normed x1_ready x1_saved mid_stat mid_aggr mid_mean_ps mid_dev mid_sq mid_var_ps mid_veps
            mid_rstd y1_ready sq_ready ss_ps ss_copied rn_ready sn_ready selfsim_ready rn_T rnT_copied
            rn_saved rn_back xn_ready hi_ready lo_ready
            stacked0 stacked1 xt1_ps xt1_copied
            tile_sim_ps tile_sim tile_top tile_rest tile_marked tile_adj half_T half_adjT
            v_sum v_tot v_rec
            v_T vT_copied v_saved v_back
            g1_ps g1_copied g1_stat g1_aggr g1_mean g1_mean_ps g1_dev g1_sq g1_var_ps g1_veps g1_rstd
            g1_scale g1_bias g1_half g1_tanh y2_ready xt2_ps xt2_copied
            g2_ps g2_copied g2_stat g2_aggr g2_mean g2_mean_ps g2_dev g2_sq g2_var_ps g2_veps g2_rstd
            g2_scale g2_bias g2_half g2_tanh y3_ready res_ready stored0 stored1""".split()
        done = {name: sem(name) for name in names}

        PREPARED = 9

        def since(name, count):
            if isinstance(count, int) and count <= 0:
                return done["prepared"], PREPARED
            return done[name], count

        def constant_first(eng, *counts):
            held = [count for count in counts if not isinstance(count, int)]
            for count in held:
                eng.compute_val(count)
            if held:
                eng.wait_ge(done["prepared"], PREPARED)

        LEAD = {"neighbours": 0, "transposes": 0, "convolve": -1, "unit": 1, "attend": 2}
        FIRST = 3

        def weave(engine, stages, i, par):
            live = []
            for stage in stages:
                b = i + LEAD[stage.__name__]
                if not isinstance(b, int) or 0 <= b < B:
                    steps = stage(b, (par + LEAD[stage.__name__]) % 2)
                    next(steps)
                    live += [(at, steps) for at in TIMES[engine][stage.__name__]]
            for _, steps in sorted(live, key=lambda e: e[0]):
                next(steps, None)

        def samples(engine, eng, *stages, last=4):
            for i in range(-3, FIRST):
                weave(engine, stages, i, i % 2)
            with eng.Fori(0, (B + 1 - last - FIRST) // 2) as k:
                weave(engine, stages, 2 * k + FIRST, 1)
                weave(engine, stages, 2 * k + FIRST + 1, 0)
            for i in range(B + 1 - last, B + 1):
                weave(engine, stages, i, i % 2)

        block = ctx.enter_context(nc.Block())

        @block.sync
        def _(sp):
            for dst, src in ((cst, constants), (vec, vectors), (wq, w_q), (wk, w_k), (wv, w_v), (wo, w_o),
                             (w1r, w_1), (w2r, w_2)):
                sp.dma_start(dst[:], src).then_inc(done["loaded_weights"], 16)

            def load(dst, signal, b, p):
                for h in range(2):
                    sp.dma_start(dst[p][h * C:(h + 1) * C, :], x[b, :, h * H:(h + 1) * H]).then_inc(done[f"{signal}{p}"], 16)

            def spread(b, row, src, dst, copied, saved, back, used):
                constant_first(sp, b + 1)
                sp.wait_ge(done[copied], b + 1)
                sp.dma_start(row[b, :, :], src[:, :]).then_inc(done[saved], 16)
                yield
                constant_first(sp, 16 * (b + 1), b)
                sp.wait_ge(done[saved], 16 * (b + 1))
                sp.wait_ge(*since(used, b))
                for h in range(2):
                    sp.dma_start(dst[h * C:(h + 1) * C, :], row[b, h * NJ:(h + 1) * NJ, :].rearrange("j q -> (j q)").unsqueeze(0)
                                 .broadcast_to([C, H])).then_inc(done[back], 16)

            def attend(b, p):
                yield
                if not isinstance(b, int) or b + 2 < B:
                    constant_first(sp, b + 1)
                    sp.wait_ge(done["y_ready"], b + 1)
                    load(xa, "xa_in", b + 2, p)
                yield
                constant_first(sp, b - 1)
                sp.wait_ge(*since("x1_ready", b - 1))
                load(xu, "xu_in", b, p)

            def unit(b, p):
                yield
                constant_first(sp, b + 1)
                sp.wait_ge(done["x1_ready"], b + 1)
                sp.dma_start(x1_kept[b, :, :], x1[:, :]).then_inc(done["x1_saved"], 16)
                yield
                yield from spread(b, rn_row, rnT, rbc, "rnT_copied", "rn_saved", "rn_back", "xn_ready")
                yield
                constant_first(sp, NT * (b - 1))
                sp.wait_ge(*since("tile_sim_ps", NT * (b - 1)))
                constant_first(sp, b + 1)
                sp.wait_ge(done["hi_ready"], b + 1)
                for h in range(2):
                    tok = slice(h * H, (h + 1) * H)
                    for dst, lo in ((hilo, 0), (hihi, 0), (hihi, C)):
                        sp.dma_start(dst[p][lo:lo + C, tok], xhi[h * C:(h + 1) * C, :]).then_inc(done[f"stacked{p}"], 16)
                constant_first(sp, b + 1)
                sp.wait_ge(done["lo_ready"], b + 1)
                for h in range(2):
                    tok = slice(h * H, (h + 1) * H)
                    for dst, lo in ((hilo, C), (lolo, 0), (lolo, C)):
                        sp.dma_start(dst[p][lo:lo + C, tok], xlo[h * C:(h + 1) * C, :]).then_inc(done[f"stacked{p}"], 16)

            def neighbours(b, p):
                yield
                constant_first(sp, 16 * (b + 1))
                sp.wait_ge(done["x1_saved"], 16 * (b + 1))
                constant_first(sp, b - 1)
                sp.wait_ge(*since("res_ready", b - 1))
                sp.dma_start(x1c[p][:, :], x1_kept[b, :, :]).then_inc(done[f"x1_back{p}"], 16)

            def convolve(b, p):
                yield
                yield from spread(b, v_row, vrT, vbc, "vT_copied", "v_saved", "v_back", "g2_copied")
                yield
                constant_first(sp, b + 1)
                sp.wait_ge(done["res_ready"], b + 1)
                for h in range(2):
                    sp.dma_start(out[b, :, h * H:(h + 1) * H], res[p][h * C:(h + 1) * C, :]).then_inc(done[f"stored{p}"], 16)

            load(xa, "xa_in", 0, 0)
            load(xa, "xa_in", 1, 1)
            samples("sync", sp, neighbours, convolve, unit, attend, last=6)
            for p in range(2):
                sp.wait_ge(done[f"stored{p}"], 32 * (B // 2))

        @block.gpsimd
        def _(pool):
            pool.memset(minus_half[:, :], -0.5).then_inc(done["prepared"], 1)
            pool.memset(w1[:, :], 0.0).then_inc(done["prepared"], 1)
            pool.memset(w2[:, :], 0.0).then_inc(done["prepared"], 1)
            pool.wait_ge(done["prepared"], 3)

            def rstd(b, tag):
                pool.wait_ge(done[f"{tag}_veps"], b + 1)
                pool.tensor_tensor(st[tag][:, 13:14], st[tag][:, 12:13], minus_half[:, 0:1], ALU.pow).then_inc(done[f"{tag}_rstd"], 1)

            def attend(b, p):
                yield
                rstd(b, "in")
                yield
                pool.wait_ge(done["q_rec"], b + 1)
                pool.wait_ge(*since("q_T", b))
                pool.tensor_tensor(qn[:, :, :], qe[:, :, :], qrec[:, :].unsqueeze(2).broadcast_to([P, NT * HEADS, D]),
                                   ALU.mult).then_inc(done["q_norm"], 1)

            def unit(b, p):
                yield
                rstd(b, "att")
                yield
                pool.wait_ge(done["att_normed"], b + 1)
                pool.wait_ge(*since("x1_saved", 16 * b))
                pool.wait_ge(*since("y1_ready", b))
                pool.wait_ge(done[f"xu_in{p}"], 16 * (b - p + 2))
                pool.tensor_tensor(x1[:, :], attn[:, :], xu[p][:, :], ALU.add).then_inc(done["x1_ready"], 1)
                yield
                rstd(b, "mid")
                yield
                pool.wait_ge(done["ss_copied"], b + 1)
                pool.wait_ge(*since("rn_T", b))
                pool.wait_ge(*since("selfsim_ready", b))
                pool.tensor_tensor(rn[:, :], ssq[:, :], minus_half[:, :], ALU.pow).then_inc(done["rn_ready"], 1)

            def neighbours(b, p):
                for r in range(NT):
                    n = NT * b + r
                    rows = slice(r * P, (r + 1) * P)
                    yield
                    constant_first(pool, n + 1)
                    pool.wait_ge(done["tile_rest"], n + 1)
                    pool.affine_select(out=rest[r % 2][:, rows], in_=rest[r % 2][:, rows], compare_op=ALU.not_equal,
                                       fill=MARK, base=0, pattern=[[-1, P]], channel_multiplier=1).then_inc(done["tile_marked"], 1)
                    pool.wait_ge(done["tile_marked"], n + 1)
                    pool.wait_ge(*since("half_T", 2 * (n - 1)))
                    pool.tensor_tensor(adj[r % 2][:, :], sim[r % 4][:, :], rest[r % 2][:, :], ALU.subtract).then_inc(done["tile_adj"], 1)

            def convolve(b, p):
                yield
                rstd(b, "g1")
                yield
                rstd(b, "g2")
                yield
                pool.wait_ge(done["y3_ready"], b + 1)
                pool.wait_ge(done[f"x1_back{p}"], 8 * (b - p + 2))
                pool.wait_ge(*since(f"stored{p}", 16 * (b - p)))
                pool.tensor_tensor(res[p][:, :], y3[:, :], x1c[p][:, :], ALU.add).then_inc(done["res_ready"], 1)

            samples("gpsimd", pool, neighbours, convolve, unit, attend)

        @block.scalar
        def _(act):
            act.wait_ge(done["u_ps"], 1)
            act.copy(u[:, :, :], pB[:, 0:HEADS * C].rearrange("c (h o) -> c h o", h=HEADS)).then_inc(done["u_ready"], 1)
            act.wait_ge(done["loaded_weights"], 16 * 8)

            def attend(b, p):
                yield
                act.wait_ge(done["k_max"], b + 1)
                act.wait_ge(*since("ek_T", b))
                act.wait_ge(*since("k_rec", b))
                act.activation(ek[:, :], pA[:, :], ACT.Exp, bias=kstat[:, 0:1], scale=1.0,
                               accum_out=kstat[:, 1:2]).then_inc(done["k_exp"], 1)
                yield
                act.wait_ge(done["yT_ps"], b + 1)
                act.wait_ge(*since("ky_ps", b))
                act.copy(yT[:, :, :], pB[:, :].rearrange("p (j q) -> p j q", j=NJ)).then_inc(done["yT_copied"], 1)
                yield
                act.wait_ge(done["ek_T"], b + 1)
                act.copy(ekT[:, :, :], pA[:, :].rearrange("p (t q) -> p t q", t=NT)).then_inc(done["ekT_copied"], 1)
                yield
                act.wait_ge(done["ky_ps"], b + 1)
                act.wait_ge(*since("m_ps", b))
                act.copy(kyT[:, :], pB[:, 0:P]).then_inc(done["ky_copied"], 1)
                yield
                act.wait_ge(done["q_sub"], b + 1)
                act.wait_ge(*since("q_norm", b))
                act.activation(qe[:, :, :], qs[:, :, :], ACT.Exp).then_inc(done["q_exp"], 1)
                yield
                act.wait_ge(done["q_T"], b + 1)
                act.wait_ge(*since("att_ps", b))
                act.copy(qh[:, :], pA[:, :]).then_inc(done["qh_copied"], 1)
                yield
                act.wait_ge(done["att_ps"], b + 1)
                act.wait_ge(*since("att_normed", b))
                act.wait_ge(*since("att_stat", b))
                act.activation(att[:, :], pB[:, :], ACT.Identity, bias=vector("b_out")).then_inc(done["att_copied"], 1)

            def unit(b, p):
                yield
                act.wait_ge(done["att_bias"], b + 1)
                act.wait_ge(*since("x1_ready", b))
                act.activation(attn[:, :], att[:, :], ACT.Identity, bias=st["att"][:, 15:16],
                               scale=st["att"][:, 14:15]).then_inc(done["att_normed"], 1)
                yield
                act.wait_ge(done["y1_ready"], b + 1)
                act.wait_ge(*since("ss_ps", b))
                act.activation(sq[:, :], y1[:, :], ACT.Square).then_inc(done["sq_ready"], 1)
                yield
                act.wait_ge(done["xn_ready"], b + 1)
                act.wait_ge(*since(f"stacked{1 - p}", 16 * 6 * (b + p)))
                act.copy(xhi[:, :], xn[p][:, :]).then_inc(done["hi_ready"], 1)

            def neighbours(b, p):
                yield
                act.wait_ge(done["xt1_ps"], b + 1)
                act.wait_ge(*since("g1_ps", b - 1))
                act.copy(xt1[p][:, :, :, :], pD[:, :].rearrange("p (j h c) -> p j h c", j=NJ, h=2)).then_inc(done["xt1_copied"], 1)
                for r in range(NT):
                    yield
                    act.wait_ge(done["tile_sim_ps"], NT * b + r + 1)
                    act.wait_ge(*since("tile_adj", NT * b + r - 3))
                    act.copy(sim[r % 4][:, :], pS[:, :]).then_inc(done["tile_sim"], 1)

            def transposes(b, p):
                for n in range(2 * (NT - 2)):
                    yield
                    copy_transposed(b, p, n // 2, n % 2)

            def copy_transposed(b, p, r, k):
                if r == 0 and k == 0:
                    act.wait_ge(*since("g2_ps", b - 1))
                act.wait_ge(done["half_T"], 2 * (NT * b + r) + k + 1)
                act.copy(adjT[p][:, NJ * k:NJ * (k + 1), r * P:(r + 1) * P], pT[:, :, :]).then_inc(done["half_adjT"], 1)

            def silu_parts(b, tag, src, half, tanh):
                act.wait_ge(done[f"{tag}_bias"], b + 1)
                act.wait_ge(*since({"g1": "y2_ready", "g2": "y3_ready"}[tag], b))
                act.activation(half[:, :], src[:, :], ACT.Identity, bias=st[tag][:, 15:16],
                               scale=st[tag][:, 14:15]).then_inc(done[f"{tag}_half"], 1)
                yield
                act.activation(tanh[:, :], src[:, :], ACT.Tanh, bias=st[tag][:, 15:16],
                               scale=st[tag][:, 14:15]).then_inc(done[f"{tag}_tanh"], 1)

            def convolve(b, p):
                for n in range(4):
                    yield
                    copy_transposed(b, p, NT - 2 + n // 2, n % 2)
                yield
                yield from silu_parts(b, "g1", g, zh, th)
                yield
                act.wait_ge(done["xt2_ps"], b + 1)
                act.wait_ge(*since("g2_ps", b))
                act.copy(xt2[:, :, :, :], pC[:, :].rearrange("p (j h c) -> p j h c", j=NJ, h=2)).then_inc(done["xt2_copied"], 1)
                yield
                yield from silu_parts(b, "g2", g2, zh2, th2)

            samples("scalar", act, neighbours, transposes, convolve, unit, attend)

        @block.vector
        def _(dve):
            dve.wait_ge(done["loaded_weights"], 16 * 8)
            dve.wait_ge(done["prepared"], 3)
            dve.tensor_scalar(mark16[:, :], ident, MARK, None, ALU.mult).then_inc(done["prepared"], 1)
            dve.tensor_copy(ident16[:, :], ident).then_inc(done["prepared"], 1)
            for h in range(2):
                c = slice(h * C, (h + 1) * C)
                dve.tensor_scalar(w1[c, c], w1r[c, :], 1.0 / XSCALE, None, ALU.mult).then_inc(done["prepared"], 1)
                dve.tensor_copy(w2[c, c], w2r[c, :]).then_inc(done["prepared"], 1)

            def stats(b, tag, src, ready, shift=None):
                dve.wait_ge(done[ready], b + 1)
                dve.wait_ge(*since(f"{tag}_aggr", b))
                dve.bn_stats(st[tag][:, 0:6], src).then_inc(done[f"{tag}_stat"], 1)
                constant_first(dve, b + 1, b, b)
                dve.wait_ge(done[f"{tag}_stat"], b + 1)
                dve.wait_ge(*since(f"{tag}_mean_ps", b))
                dve.wait_ge(*since(f"{tag}_sq", b))
                dve.bn_aggr(st[tag][:, 6:8], st[tag][:, 0:6]).then_inc(done[f"{tag}_aggr"], 1)
                if shift is not None:
                    dve.wait_ge(done[f"{tag}_aggr"], b + 1)
                    dve.tensor_tensor(st[tag][:, 6:7], st[tag][:, 6:7], shift, ALU.add).then_inc(done[f"{tag}_mean"], 1)

            def deviation(b, tag, ps):
                dve.wait_ge(done[f"{tag}_mean_ps"], b + 1)
                dve.tensor_scalar(st[tag][:, 8:9], ps[:, 0:1], -1.0, None, ALU.mult)
                dve.tensor_tensor(st[tag][:, 9:10], st[tag][:, 6:7], ps[:, 0:1], ALU.subtract).then_inc(done[f"{tag}_dev"], 1)
                dve.wait_ge(done[f"{tag}_dev"], b + 1)
                dve.wait_ge(*since(f"{tag}_var_ps", b))
                dve.scalar_tensor_tensor(out=st[tag][:, 10:11], in0=st[tag][:, 9:10], scalar=st[tag][:, 9:10],
                                         in1=st[tag][:, 7:8], op0=ALU.mult, op1=ALU.add).then_inc(done[f"{tag}_sq"], 1)

            def variance(b, tag, ps):
                dve.wait_ge(done[f"{tag}_var_ps"], b + 1)
                dve.wait_ge(*since(f"{tag}_rstd", b))
                dve.tensor_scalar(st[tag][:, 12:13], ps[:, 1:2], EPS, None, ALU.add).then_inc(done[f"{tag}_veps"], 1)

            def affine(b, tag, weight, bias, half, shift=None):
                f = 0.5 if half else 1.0
                t = st[tag]
                dve.wait_ge(done[f"{tag}_rstd"], b + 1)
                dve.wait_ge(*since({"att": "att_normed", "g1": "g1_tanh", "g2": "g2_tanh"}[tag], b))
                dve.tensor_scalar(t[:, 14:15], t[:, 13:14], weight, f, ALU.mult, ALU.mult).then_inc(done[f"{tag}_scale"], 1)
                if shift is not None:
                    dve.tensor_tensor(t[:, 16:17], t[:, 8:9], shift, ALU.add)
                else:
                    dve.tensor_copy(t[:, 16:17], t[:, 8:9])
                dve.tensor_scalar(t[:, 17:18], bias, f, None, ALU.mult).then_inc(done[f"{tag}_scale"], 1)
                dve.wait_ge(done[f"{tag}_scale"], 2 * (b + 1))
                dve.scalar_tensor_tensor(out=t[:, 15:16], in0=t[:, 16:17], scalar=t[:, 14:15], in1=t[:, 17:18],
                                         op0=ALU.mult, op1=ALU.add).then_inc(done[f"{tag}_bias"], 1)

            def attend(b, p):
                yield
                dve.wait_ge(done[f"xa_in{p}"], 16 * (b - p + 2))
                dve.wait_ge(*since("in_aggr", b))
                dve.bn_stats(st["in"][:, 0:6], xa[p][:, :]).then_inc(done["in_stat"], 1)
                constant_first(dve, b + 1, b, b)
                dve.wait_ge(done["in_stat"], b + 1)
                dve.wait_ge(*since("in_mean_ps", b))
                dve.wait_ge(*since("in_sq", b))
                dve.bn_aggr(st["in"][:, 6:8], st["in"][:, 0:6]).then_inc(done["in_aggr"], 1)
                yield
                deviation(b, "in", pB)
                yield
                variance(b, "in", pB)
                yield
                dve.wait_ge(done["in_rstd"], b + 1)
                dve.wait_ge(*since("q_ps", b))
                dve.tensor_scalar(y[:, :], xa[p][:, :], st["in"][:, 8:9], st["in"][:, 13:14], ALU.add,
                                  ALU.mult).then_inc(done["y_ready"], 1)
                yield
                dve.wait_ge(done["k_ps"], b + 1)
                dve.tensor_reduce(kstat[:, 0:1], pA[:, :], AX.X, ALU.max, negate=True).then_inc(done["k_max"], 1)
                yield
                dve.wait_ge(done["k_exp"], b + 1)
                dve.reciprocal(kstat[:, 2:3], kstat[:, 1:2]).then_inc(done["k_rec"], 1)
                yield
                dve.wait_ge(done["q_ps"], b + 1)
                q_ps = pA[:, :].rearrange("p (g d) -> p g d", d=D)
                dve.tensor_reduce(qmax[:, :], q_ps, AX.X, ALU.max).then_inc(done["q_max"], 1)
                yield
                dve.wait_ge(done["q_max"], b + 1)
                dve.wait_ge(*since("q_exp", b))
                dve.tensor_tensor(qs[:, :, :], q_ps, qmax[:, :].unsqueeze(2).broadcast_to([P, NT * HEADS, D]),
                                  ALU.subtract).then_inc(done["q_sub"], 1)
                yield
                dve.wait_ge(done["m_ps"], b + 1)
                dve.wait_ge(done["k_rec"], b + 1)
                dve.wait_ge(*since("att_ps", b))
                dve.tensor_scalar(mT[:, :], pB[:, 256:256 + C], kstat[:, 2:3], SCALE, ALU.mult, ALU.mult).then_inc(done["m_copied"], 1)
                yield
                dve.wait_ge(done["q_exp"], b + 1)
                dve.tensor_reduce(qsum[:, :], qe[:, :, :], AX.X, ALU.add).then_inc(done["q_sum"], 1)
                yield
                dve.wait_ge(done["q_sum"], b + 1)
                dve.wait_ge(*since("q_norm", b))
                dve.reciprocal(qrec[:, :], qsum[:, :]).then_inc(done["q_rec"], 1)

            def unit(b, p):
                yield
                stats(b, "att", att[:, :], "att_copied")
                yield
                deviation(b, "att", pD)
                yield
                variance(b, "att", pD)
                yield
                affine(b, "att", vector("gn_weight"), vector("gn_bias"), False)
                yield
                stats(b, "mid", x1[:, :], "x1_ready")
                yield
                deviation(b, "mid", pD)
                yield
                variance(b, "mid", pD)
                yield
                dve.wait_ge(done["mid_rstd"], b + 1)
                dve.wait_ge(*since("xn_ready", b))
                dve.wait_ge(*since("sq_ready", b))
                dve.tensor_scalar(y1[:, :], x1[:, :], st["mid"][:, 8:9], st["mid"][:, 13:14], ALU.add,
                                  ALU.mult).then_inc(done["y1_ready"], 1)
                yield
                dve.wait_ge(done["ss_ps"], b + 1)
                dve.wait_ge(*since("rn_ready", b))
                dve.wait_ge(*since("sn_ready", b))
                dve.tensor_copy(ss[:, :], pD[:, 0:NT])
                dve.tensor_scalar(ssq[:, :], pD[:, 0:NT], 1e-24, 1.0 / SSCALE, ALU.max, ALU.mult).then_inc(done["ss_copied"], 1)
                yield
                dve.wait_ge(done["rn_ready"], b + 1)
                dve.wait_ge(done["ss_copied"], b + 1)
                dve.wait_ge(*since("selfsim_ready", b))
                dve.tensor_tensor(sn[:, :], ss[:, :], rn[:, :], ALU.mult).then_inc(done["sn_ready"], 1)
                yield
                dve.wait_ge(done["rn_T"], b + 1)
                dve.wait_ge(*since("rn_saved", 16 * b))
                dve.tensor_copy(rnT[:, :], pD[0:NT, P:2 * P]).then_inc(done["rnT_copied"], 1)
                yield
                dve.wait_ge(done["rn_back"], 32 * (b + 1))
                dve.wait_ge(*since("xt1_ps", b - 1))
                dve.wait_ge(*since("hi_ready", b - 1))
                dve.tensor_tensor(xn[p][:, :], y1[:, :], rbc[:, :], ALU.mult).then_inc(done["xn_ready"], 1)
                yield
                dve.wait_ge(done["hi_ready"], b + 1)
                dve.wait_ge(done["xn_ready"], b + 1)
                dve.wait_ge(*since(f"stacked{1 - p}", 16 * 6 * (b + p)))
                dve.tensor_tensor(xlo[:, :], xn[p][:, :], xhi[:, :], ALU.subtract).then_inc(done["lo_ready"], 1)
                yield
                dve.wait_ge(done["sn_ready"], b + 1)
                dve.wait_ge(*since("v_tot", b - 1))
                dve.tensor_tensor(selfsim[p][:, :], sn[:, :], rn[:, :], ALU.mult).then_inc(done["selfsim_ready"], 1)

            def neighbours(b, p):
                for r in range(NT):
                    n = NT * b + r
                    yield
                    constant_first(dve, n + 1, b)
                    dve.wait_ge(done["tile_sim"], n + 1)
                    dve.wait_ge(*since("v_sum", b))
                    dve.max(top[:, r, :], sim[r % 4][:, :]).then_inc(done["tile_top"], 1)
                    yield
                    constant_first(dve, n + 1, n - 1)
                    dve.wait_ge(done["tile_top"], n + 1)
                    dve.wait_ge(*since("tile_adj", n - 1))
                    dve.match_replace(out=rest[r % 2][:, :], in_to_replace=top[:, r, :], in_values=sim[r % 4][:, :],
                                      imm_value=0.0).then_inc(done["tile_rest"], 1)
                yield
                dve.tensor_reduce(vsum[:, :], top[:, :, :], AX.X, ALU.add).then_inc(done["v_sum"], 1)
                dve.wait_ge(done["v_sum"], b + 1)
                dve.wait_ge(done["selfsim_ready"], b + 1)
                dve.scalar_tensor_tensor(out=vtot[:, :], in0=vsum[:, :], scalar=1e-6 * SSCALE, in1=selfsim[p][:, :],
                                         op0=ALU.add, op1=ALU.add).then_inc(done["v_tot"], 1)
                dve.wait_ge(done["v_tot"], b + 1)
                dve.wait_ge(*since("v_T", b - 1))
                dve.reciprocal(vrec[p][:, :], vtot[:, :]).then_inc(done["v_rec"], 1)

            def gcn(b, tag, first, dst, tanh, half, act_out, act_name, bias, gamma, beta):
                yield
                dve.wait_ge(done[f"{tag}_ps"], b + 1)
                dve.wait_ge(done["v_back"], 32 * (b + 1))
                dve.wait_ge(*since(f"{tag}_tanh", b))
                dve.wait_ge(*since(f"{tag}_stat", b))
                dve.tensor_tensor(dst[:, :], pC[:, :], vbc[:, :], ALU.mult).then_inc(done[f"{tag}_copied"], 1)
                yield
                stats(b, tag, dst[:, :], f"{tag}_copied", shift=vector(bias))
                yield
                deviation(b, tag, pC)
                yield
                variance(b, tag, pC)
                yield
                affine(b, tag, vector(gamma), vector(beta), True, shift=vector(bias))
                yield
                dve.wait_ge(done[f"{tag}_tanh"], b + 1)
                if tag == "g1":
                    dve.wait_ge(*since("xt2_ps", b))
                else:
                    dve.wait_ge(*since("res_ready", b))
                dve.scalar_tensor_tensor(out=act_out[:, :], in0=tanh[:, :], scalar=1.0, in1=half[:, :], op0=ALU.add,
                                         op1=ALU.mult).then_inc(done[act_name], 1)

            def convolve(b, p):
                yield
                dve.wait_ge(done["v_T"], b + 1)
                dve.wait_ge(*since("v_saved", 16 * b))
                dve.tensor_copy(vrT[:, :], pC[0:NT, 0:P]).then_inc(done["vT_copied"], 1)
                yield from gcn(b, "g1", 12, g, th, zh, y2, "y2_ready", "b1", "gamma1", "beta1")
                yield from gcn(b, "g2", 28, g2, th2, zh2, y3, "y3_ready", "b2", "gamma2", "beta2")

            samples("vector", dve, neighbours, convolve, unit, attend)

        @block.tensor
        def _(pe):
            pe.wait_ge(done["loaded_weights"], 16 * 8)
            pe.wait_ge(done["prepared"], PREPARED)
            for h in range(HEADS):
                for c in (slice(0, C), slice(C, P)):
                    mm = pe.matmul(pB[c, h * C:(h + 1) * C], wv[:, h, :], wo[:, h, :], start=True, stop=True)
            mm.then_inc(done["u_ps"], 1)
            pe.wait_ge(done["u_ready"], 1)

            def average(b, tag, ps, avg, mean_ready):
                pe.wait_ge(done[mean_ready], b + 1)
                pe.matmul(ps[:, 0:1], const(avg), st[tag][:, 6:7], start=True, stop=True).then_inc(done[f"{tag}_mean_ps"], 1)

            def average_sq(b, tag, ps, avg):
                pe.wait_ge(done[f"{tag}_sq"], b + 1)
                pe.matmul(ps[:, 1:2], const(avg), st[tag][:, 10:11], start=True, stop=True).then_inc(done[f"{tag}_var_ps"], 1)

            def token_block(t):
                h, j = divmod(t, NJ)
                return slice(h * C, (h + 1) * C), slice(j * P, (j + 1) * P)

            def attend(b, p):
                yield
                pe.wait_ge(*since("att_copied", b))
                average(b, "in", pB, "avg_pair", "in_aggr")
                yield
                average_sq(b, "in", pB, "avg_pair")
                yield
                pe.wait_ge(done["y_ready"], b + 1)
                pe.wait_ge(*since("qh_copied", b))
                for h in range(2):
                    c = slice(h * C, (h + 1) * C)
                    mm = pe.matmul(pA[:, h * H:(h + 1) * H], wk[c, :], y[c, :], start=True, stop=True)
                mm.then_inc(done["k_ps"], 1)
                yield
                pe.wait_ge(done["in_veps"], b + 1)
                for j in range(NJ):
                    mm = pe.transpose(pB[:, j * P:(j + 1) * P], y[:, j * P:(j + 1) * P], ident)
                mm.then_inc(done["yT_ps"], 1)
                yield
                pe.wait_ge(done["k_exp"], b + 1)
                for t in range(NT):
                    mm = pe.transpose(pA[:, t * P:(t + 1) * P], ek[:, t * P:(t + 1) * P], ident)
                mm.then_inc(done["ek_T"], 1)
                yield
                pe.wait_ge(done["ekT_copied"], b + 1)
                for t in range(NT):
                    c, tok = token_block(t)
                    mm = pe.matmul(pA[:, t * P:(t + 1) * P], y[c, tok], wq[c, :], start=True, stop=True)
                mm.then_inc(done["q_ps"], 1)
                yield
                pe.wait_ge(done["yT_copied"], b + 1)
                for j in range(NJ):
                    for h in range(2):
                        c = slice(h * C, (h + 1) * C)
                        mm = pe.matmul(pB[c, 0:P], yT[:, j, c], ekT[:, h * NJ + j, :], start=(j == 0), stop=(j == NJ - 1))
                mm.then_inc(done["ky_ps"], 1)
                yield
                constant_first(pe, b + 1)
                pe.wait_ge(done["ky_copied"], b + 1)
                for h in range(HEADS):
                    mm = pe.matmul(pB[h * D:(h + 1) * D, 256:256 + C], kyT[:, h * D:(h + 1) * D], u[:, h, :], start=True, stop=True)
                mm.then_inc(done["m_ps"], 1)
                yield
                pe.wait_ge(done["q_norm"], b + 1)
                for t in range(NT):
                    mm = pe.transpose(pA[:, t * P:(t + 1) * P], qn[:, t * HEADS:(t + 1) * HEADS, :], ident)
                mm.then_inc(done["q_T"], 1)
                yield
                pe.wait_ge(done["qh_copied"], b + 1)
                pe.wait_ge(done["m_copied"], b + 1)
                for h in range(2):
                    mm = pe.matmul(pB[h * C:(h + 1) * C, :], mT[:, :], qh[:, h * H:(h + 1) * H], start=True, stop=True)
                mm.then_inc(done["att_ps"], 1)

            def unit(b, p):
                yield
                pe.wait_ge(*since("xt1_copied", b))
                average(b, "att", pD, "avg_sample", "att_aggr")
                yield
                average_sq(b, "att", pD, "avg_sample")
                yield
                pe.wait_ge(done["att_veps"], b + 1)
                average(b, "mid", pD, "avg_pair", "mid_aggr")
                yield
                average_sq(b, "mid", pD, "avg_pair")
                yield
                pe.wait_ge(done["sq_ready"], b + 1)
                pe.wait_ge(done["mid_veps"], b + 1)
                for j in range(NJ):
                    mm = pe.matmul(pD[:, j:j + NJ + 1:NJ], sq[:, j * P:(j + 1) * P], const("halves"), start=True, stop=True)
                mm.then_inc(done["ss_ps"], 1)
                yield
                pe.wait_ge(done["rn_ready"], b + 1)
                pe.transpose(pD[0:NT, P:2 * P], rn[:, :], ident).then_inc(done["rn_T"], 1)

            def neighbours(b, p):
                yield
                pe.wait_ge(done["xn_ready"], b + 1)
                for j in range(NJ):
                    mm = pe.matmul(pD[:, j * P:(j + 1) * P], xn[p][:, j * P:(j + 1) * P], w1[:, :], start=True, stop=True)
                mm.then_inc(done["xt1_ps"], 1)
                pe.wait_ge(done[f"stacked{p}"], 16 * 6 * (b - p + 2))
                for r in range(NT):
                    yield
                    pe.wait_ge(*since("tile_sim", NT * b + r))
                    rows = slice(r * P, (r + 1) * P)
                    for h in range(2):
                        tok = slice(h * H, (h + 1) * H)
                        pe.matmul(pS[:, tok], hilo[p][:, rows], hihi[p][:, tok], start=True, stop=False)
                        if r // NJ == h:
                            pe.matmul(pS[:, rows], ident16[:, :], mark16[:, :], start=False, stop=False,
                                      skip_group_check=True)
                        mm = pe.matmul(pS[:, tok], hilo[p][:, rows], lolo[p][:, tok], start=False, stop=True)
                    mm.then_inc(done["tile_sim_ps"], 1)

            def transposes(b, p):
                for n in range(2 * (NT - 2)):
                    yield
                    transpose_half(b, n // 2, n % 2)

            def transpose_half(b, r, k):
                pe.wait_ge(done["tile_adj"], NT * b + r + 1)
                pe.wait_ge(*since("half_adjT", 2 * (NT * b + r) + k))
                for j in range(NJ):
                    t = NJ * k + j
                    mm = pe.transpose(pT[:, j, :], adj[r % 2][:, t * P:(t + 1) * P], ident)
                mm.then_inc(done["half_T"], 1)

            def aggregate(xt, p, first, signal):
                for t in range(NT):
                    yield
                    for h in range(2):
                        mm = pe.matmul(pC[h * C:(h + 1) * C, :], xt[:, t % NJ, t // NJ, :], adjT[p][:, t, h * H:(h + 1) * H],
                                       start=(t == 0), stop=(t == NT - 1))
                mm.then_inc(done[signal], 1)

            def convolve(b, p):
                for n in range(4):
                    yield
                    transpose_half(b, NT - 2 + n // 2, n % 2)
                yield
                pe.wait_ge(done["v_rec"], b + 1)
                pe.wait_ge(*since("g2_veps", b))
                pe.transpose(pC[0:NT, 0:P], vrec[p][:, :], ident).then_inc(done["v_T"], 1)
                yield
                pe.wait_ge(done["vT_copied"], b + 1)
                pe.wait_ge(done["xt1_copied"], b + 1)
                pe.wait_ge(done["half_adjT"], 2 * NT * (b + 1))
                yield from aggregate(xt1[p], p, 4, "g1_ps")
                yield
                pe.wait_ge(done["g1_copied"], b + 1)
                average(b, "g1", pC, "avg_group", "g1_mean")
                yield
                average_sq(b, "g1", pC, "avg_group")
                yield
                pe.wait_ge(done["y2_ready"], b + 1)
                pe.wait_ge(done["g1_veps"], b + 1)
                for j in range(NJ):
                    mm = pe.matmul(pC[:, j * P:(j + 1) * P], y2[:, j * P:(j + 1) * P], w2[:, :], start=True, stop=True)
                mm.then_inc(done["xt2_ps"], 1)
                yield
                pe.wait_ge(done["xt2_copied"], b + 1)
                yield from aggregate(xt2, p, 20, "g2_ps")
                yield
                pe.wait_ge(done["g2_copied"], b + 1)
                average(b, "g2", pC, "avg_group", "g2_mean")
                yield
                average_sq(b, "g2", pC, "avg_group")

            samples("tensor", pe, neighbours, transposes, convolve, unit, attend)


def kernel(**inputs):
    import concourse.bacc as bacc
    from concourse.bass_utils import run_bass_kernel_spmd as run

    a = {n: np.asarray(v) for n, v in inputs.items()}
    x = a["x"]
    B, C, Hh, Ww = x.shape
    w_qkv = a["L0_conv_w_qkv"]
    hid = w_qkv.shape[0] // 3

    def twice(m):
        return np.ascontiguousarray(np.concatenate([m, m], axis=0))

    cols = [a["L0_conv_b_out"], a["L0_conv_gn_weight"], a["L0_conv_gn_bias"], a["L1_conv_b1"], a["L1_conv_gamma1"],
            a["L1_conv_beta1"], a["L1_conv_b2"], a["L1_conv_gamma2"], a["L1_conv_beta2"]]
    arrays = {
        "x": np.ascontiguousarray(x.reshape(B, C, Hh * Ww)),
        "w_q": twice(w_qkv[0:hid].T),
        "w_k": twice(w_qkv[hid:2 * hid].T),
        "w_v": np.ascontiguousarray(w_qkv[2 * hid:].reshape(HEADS, -1, C).transpose(1, 0, 2)),
        "w_o": np.ascontiguousarray(a["L0_conv_w_out"].T.reshape(HEADS, -1, C).transpose(1, 0, 2)),
        "w_1": twice(a["L1_conv_w1"]),
        "w_2": twice(a["L1_conv_w2"]),
        "vectors": twice(np.stack(cols, axis=1)),
        "constants": shape_constants(C),
    }
    nc = bacc.Bacc("TRN2", target_bir_lowering=False, num_devices=1)
    args = [nc.dram_tensor(n, v.shape, mybir.dt.from_np(v.dtype), kind="ExternalInput").ap() for n, v in arrays.items()]
    out = nc.dram_tensor("out", (B, C, Hh * Ww), F32, kind="ExternalOutput").ap()
    build(nc, *args, out)
    r = run(nc, [arrays], core_ids=[0])
    return r.results[0]["out"].reshape(B, C, Hh, Ww)
```

```python
from contextlib import ExitStack

import numpy as np

import concourse.bass as bass
from concourse import mybir

ALU = mybir.AluOpType
ACT = mybir.ActivationFunctionType
AX = mybir.AxisListType
F32 = mybir.dt.float32
F16 = mybir.dt.float16

P = 128
HEADS = 4
TOP = 8
XSCALE = 64.0
SSCALE = XSCALE * XSCALE
MARK = -2.5 * SSCALE
EPS = 1e-5

CONST_PARTS = [("ident", P), ("avg_pair", P), ("avg_sample", P), ("avg_group", P), ("halves", 2)]
WEIGHT_PARTS = [("w_q", P), ("w_k", P), ("w_1", 64), ("w_2", 64)]
VECTORS = ["b_out", "gn_weight", "gn_bias", "b1", "gamma1", "beta1", "b2", "gamma2", "beta2"]
PACKED = CONST_PARTS + WEIGHT_PARTS + [(name, 1) for name in VECTORS]


TIMES = {
    "sync": {
        "neighbours": [103],
        "convolve": [64, 65, 788],
        "unit": [16, 186, 187, 247],
        "attend": [104, 396],
    },
    "gpsimd": {
        "neighbours": [156, 239, 414, 424, 457, 543, 599, 670],
        "convolve": [289, 585, 768],
        "unit": [0, 1, 201, 259],
        "attend": [2, 488],
    },
    "scalar": {
        "neighbours": [5, 14, 36, 160, 287, 339, 392, 436, 546],
        "transposes": [289, 347, 348, 369, 470, 514, 521, 522, 555, 564, 596, 772],
        "convolve": [34, 35, 112, 120, 360, 368, 411, 617, 703],
        "unit": [134, 268, 442],
        "attend": [248, 284, 293, 396, 422, 543, 570],
    },
    "vector": {
        "neighbours": [15, 22, 65, 121, 136, 215, 317, 343, 395, 427, 436, 486, 487, 488, 672, 732, 740],
        "convolve": [16, 262, 273, 295, 325, 348, 414, 506, 540, 564, 585, 701, 751],
        "unit": [1, 2, 4, 17, 106, 129, 146, 170, 288, 327, 380, 449, 476, 563],
        "attend": [3, 57, 66, 107, 150, 293, 403, 433, 454, 468, 469],
    },
    "tensor": {
        "neighbours": [0, 1, 10, 60, 282, 393, 497, 605, 734],
        "transposes": [296, 392, 435, 522, 554, 558, 673, 698, 737, 738, 753, 796],
        "convolve": [2, 4, 19, 37, 40, 69, 71, 72, 73, 75, 76, 212, 213, 225, 364, 394, 576, 614, 635, 636, 637, 646,
                    669, 670, 671, 672, 736, 745],
        "unit": [8, 13, 93, 144, 325, 441],
        "attend": [42, 74, 132, 231, 352, 464, 546, 609, 702, 748],
    },
}


def column_of(parts, name):
    at = 0
    for n, width in parts:
        if n == name:
            return at, at + width
        at += width


def shape_constants(C):
    p = np.arange(P)
    channel = p % C
    out = {"ident": np.eye(P)}
    for name, size in (("avg_pair", 2), ("avg_sample", C), ("avg_group", C // 4)):
        same = channel[:, None] // size == channel[None, :] // size
        out[name] = same / same.sum(1, keepdims=True)
    out["halves"] = np.arange(P)[:, None] // C == np.arange(2)[None, :]
    return np.concatenate([out[n] for n, _ in CONST_PARTS], axis=1).astype(np.float32)


def build(nc, x, packed, w_vo, out):
    B, C, N = x.shape
    H = N // 2
    NT = N // P
    NJ = H // P
    D = P // HEADS
    SCALE = float(D) ** -0.5
    assert C == 64 and 2 * C == P and H == 512

    ctx = ExitStack()
    with ctx:
        def sb(name, shape, dt=F32):
            return ctx.enter_context(nc.sbuf_tensor(name, shape, dt))

        def sem(name):
            return ctx.enter_context(nc.semaphore(name))

        cst = sb("cst", [P, packed.shape[1]])
        wvo = sb("wvo", [D, 2, HEADS, C])
        w1 = sb("w1", [P, P])
        w2 = sb("w2", [P, P])
        u = sb("u", [P, HEADS, C])
        ident16 = sb("ident16", [P, P], F16)
        mark16 = sb("mark16", [P, P], F16)
        minus_half = sb("minus_half", [P, NT])

        def const(name):
            a, b = column_of(PACKED, name)
            return cst[:, a:b]

        def vector(name):
            return const(name)

        ident = const("ident")

        xa = [sb(f"xa{i}", [P, H]) for i in range(2)]
        y = sb("y", [P, H])
        ek = sb("ek", [P, N])
        ekT = sb("ekT", [P, NT, P])
        yT = sb("yT", [P, NJ, P])
        kyT = sb("kyT", [P, P])
        mT = sb("mT", [P, C])
        qs = sb("qs", [P, NT * HEADS, D])
        qe = sb("qe", [P, NT * HEADS, D])
        qn = sb("qn", [P, NT * HEADS, D])
        qh = sb("qh", [P, N])
        att = sb("att", [P, H])

        xu = [sb(f"xu{i}", [P, H]) for i in range(2)]
        attn = sb("attn", [P, H])
        x1 = sb("x1", [P, H])
        y1 = sb("y1", [P, H])
        sq = sb("sq", [P, H])
        xn = [sb(f"xn{i}", [P, H]) for i in range(2)]
        xhi = sb("xhi", [P, H], F16)
        xlo = sb("xlo", [P, H], F16)
        hilo = [sb(f"hilo{i}", [P, N], F16) for i in range(2)]
        hihi = [sb(f"hihi{i}", [P, N], F16) for i in range(2)]
        lolo = [sb(f"lolo{i}", [P, N], F16) for i in range(2)]
        st = {n: sb(f"st_{n}", [P, 24]) for n in ("in", "att", "mid", "g1", "g2")}
        kstat = sb("kstat", [P, 4])
        qmax = sb("qmax", [P, NT * HEADS])
        qsum = sb("qsum", [P, NT * HEADS])
        qrec = sb("qrec", [P, NT * HEADS])
        ss = sb("ss", [P, NT])
        ssq = sb("ssq", [P, NT])
        rn = sb("rn", [P, NT])
        sn = sb("sn", [P, NT])
        selfsim = [sb(f"selfsim{i}", [P, NT]) for i in range(2)]
        rnT = sb("rnT", [NT, P])
        rbc = sb("rbc", [P, H])

        x1c = [sb(f"x1c{i}", [P, H]) for i in range(2)]
        xt1 = [sb(f"xt1_{i}", [P, NJ, 2, C]) for i in range(2)]
        sim = [sb(f"sim{i}", [P, N]) for i in range(4)]
        rest = [sb(f"rest{i}", [P, N]) for i in range(2)]
        adj = [sb(f"adj{i}", [P, N]) for i in range(2)]
        top = sb("top", [P, NT, TOP])
        adjT = [sb(f"adjT{i}", [P, NT, N]) for i in range(2)]
        vsum = sb("vsum", [P, NT])
        vtot = sb("vtot", [P, NT])
        vrec = [sb(f"vrec{i}", [P, NT]) for i in range(2)]

        vrT = sb("vrT", [NT, P])
        vbc = sb("vbc", [P, H])
        g = sb("g", [P, H])
        zh = sb("zh", [P, H])
        th = sb("th", [P, H])
        y2 = sb("y2", [P, H])
        xt2 = sb("xt2", [P, NJ, 2, C])
        g2 = sb("g2", [P, H])
        zh2 = sb("zh2", [P, H])
        th2 = sb("th2", [P, H])
        y3 = sb("y3", [P, H])
        res = [sb(f"res{i}", [P, H]) for i in range(2)]

        x1_kept = nc.dram_tensor("x1_kept", (B, P, H), F32, kind="Internal").ap()
        rn_row = nc.dram_tensor("rn_row", (B, NT, P), F32, kind="Internal").ap()
        v_row = nc.dram_tensor("v_row", (B, NT, P), F32, kind="Internal").ap()

        pS = ctx.enter_context(nc.psum_tensor("pS", [P, N], F32))
        pT = ctx.enter_context(nc.psum_tensor("pT", [P, 2, NJ, P], F32))
        pA = ctx.enter_context(nc.psum_tensor("pA", [P, N], F32))
        pB = ctx.enter_context(nc.psum_tensor("pB", [P, H], F32))
        pC = ctx.enter_context(nc.psum_tensor("pC", [P, H], F32))

        names = """loaded_weights prepared u_ps u_ready xa_in0 xa_in1 xu_in0 xu_in1 x1_back0 x1_back1 in_stat
            in_aggr in_mean_ps in_dev in_sq in_var_ps in_veps in_rstd y_ready k_ps k_max k_exp ek_T
            ekT_copied yT_ps yT_copied ky_ps ky_copied k_rec m_ps m_copied q_ps q_max q_sub q_exp q_sum
            q_rec q_norm q_T qh_copied att_ps att_copied att_stat att_aggr att_mean_ps att_dev att_sq
            att_var_ps att_veps att_rstd att_scale att_bias att_normed x1_ready x1_saved mid_stat mid_aggr
            mid_mean_ps mid_dev mid_sq mid_var_ps mid_veps mid_rstd y1_ready sq_ready ss_ps ss_copied
            rn_ready sn_ready selfsim_ready rn_T rnT_copied rn_saved rn_back xn_ready hi_ready lo_ready
            stacked0 stacked1 xt1_ps xt1_copied tile_sim_ps tile_sim tile_top tile_rest tile_marked tile_adj
            half_T half_adjT v_sum v_tot v_rec v_T vT_copied v_saved v_back g1_ps g1_copied g1_stat g1_aggr
            g1_mean g1_mean_ps g1_dev g1_sq g1_var_ps g1_veps g1_rstd g1_scale g1_bias g1_half g1_tanh
            y2_ready xt2_ps xt2_copied g2_ps g2_copied g2_stat g2_aggr g2_mean g2_mean_ps g2_dev g2_sq
            g2_var_ps g2_veps g2_rstd g2_scale g2_bias g2_half g2_tanh y3_ready res_ready stored0 stored1""".split()
        done = {name: sem(name) for name in names}

        PREPARED = 9

        def since(name, count):
            if isinstance(count, int) and count <= 0:
                return done["prepared"], PREPARED
            return done[name], count

        def of_next(b, n):
            return min(b + n + 1, B) if isinstance(b, int) else b + n + 1

        def constant_first(eng, *counts):
            held = [count for count in counts if not isinstance(count, int)]
            for count in held:
                eng.compute_val(count)
            if held:
                eng.wait_ge(done["prepared"], PREPARED)

        LEAD = {"neighbours": 0, "transposes": 0, "convolve": -1, "unit": 1, "attend": 2}
        FIRST = 3

        def weave(engine, stages, i, par):
            live = []
            for stage in stages:
                b = i + LEAD[stage.__name__]
                if not isinstance(b, int) or 0 <= b < B:
                    steps = stage(b, (par + LEAD[stage.__name__]) % 2)
                    next(steps)
                    live += [(at, steps) for at in TIMES[engine][stage.__name__]]
            for _, steps in sorted(live, key=lambda e: e[0]):
                next(steps, None)

        def samples(engine, eng, *stages, last=4):
            for i in range(-3, FIRST):
                weave(engine, stages, i, i % 2)
            with eng.Fori(0, (B + 1 - last - FIRST) // 2) as k:
                weave(engine, stages, 2 * k + FIRST, 1)
                weave(engine, stages, 2 * k + FIRST + 1, 0)
            for i in range(B + 1 - last, B + 1):
                weave(engine, stages, i, i % 2)

        block = ctx.enter_context(nc.Block())

        @block.sync
        def _(sp):
            def load(dst, signal, b, p):
                for h in range(2):
                    sp.dma_start(dst[p][h * C:(h + 1) * C, :], x[b, :, h * H:(h + 1) * H]).then_inc(done[f"{signal}{p}"], 16)

            def spread(b, row, src, dst, copied, saved, back, used):
                constant_first(sp, b + 1)
                sp.wait_ge(done[copied], b + 1)
                sp.dma_start(row[b, :, :], src[:, :]).then_inc(done[saved], 16)
                yield
                constant_first(sp, 16 * (b + 1), b)
                sp.wait_ge(done[saved], 16 * (b + 1))
                sp.wait_ge(*since(used, b))
                for h in range(2):
                    sp.dma_start(dst[h * C:(h + 1) * C, :], row[b, h * NJ:(h + 1) * NJ, :].rearrange("j q -> (j q)").unsqueeze(0)
                                 .broadcast_to([C, H])).then_inc(done[back], 16)

            def attend(b, p):
                yield
                if not isinstance(b, int) or b + 2 < B:
                    constant_first(sp, b + 1)
                    sp.wait_ge(done["y_ready"], b + 1)
                    load(xa, "xa_in", b + 2, p)
                yield
                constant_first(sp, b - 1)
                sp.wait_ge(*since("x1_ready", b - 1))
                load(xu, "xu_in", b, p)

            def unit(b, p):
                yield
                constant_first(sp, b + 1)
                sp.wait_ge(done["x1_ready"], b + 1)
                sp.dma_start(x1_kept[b, :, :], x1[:, :]).then_inc(done["x1_saved"], 16)
                yield
                yield from spread(b, rn_row, rnT, rbc, "rnT_copied", "rn_saved", "rn_back", "xn_ready")
                yield
                constant_first(sp, NT * (b - 1))
                sp.wait_ge(*since("tile_sim_ps", NT * (b - 1)))
                constant_first(sp, b + 1)
                sp.wait_ge(done["hi_ready"], b + 1)
                for h in range(2):
                    tok = slice(h * H, (h + 1) * H)
                    for dst, lo in ((hilo, 0), (hihi, 0), (hihi, C)):
                        sp.dma_start(dst[p][lo:lo + C, tok], xhi[h * C:(h + 1) * C, :]).then_inc(done[f"stacked{p}"], 16)
                constant_first(sp, b + 1)
                sp.wait_ge(done["lo_ready"], b + 1)
                for h in range(2):
                    tok = slice(h * H, (h + 1) * H)
                    for dst, lo in ((hilo, C), (lolo, 0), (lolo, C)):
                        sp.dma_start(dst[p][lo:lo + C, tok], xlo[h * C:(h + 1) * C, :]).then_inc(done[f"stacked{p}"], 16)

            def neighbours(b, p):
                yield
                constant_first(sp, 16 * (b + 1))
                sp.wait_ge(done["x1_saved"], 16 * (b + 1))
                constant_first(sp, b - 1)
                sp.wait_ge(*since("res_ready", b - 1))
                sp.dma_start(x1c[p][:, :], x1_kept[b, :, :]).then_inc(done[f"x1_back{p}"], 16)

            def convolve(b, p):
                yield
                yield from spread(b, v_row, vrT, vbc, "vT_copied", "v_saved", "v_back", "g2_copied")
                yield
                constant_first(sp, b + 1)
                sp.wait_ge(done["res_ready"], b + 1)
                for h in range(2):
                    sp.dma_start(out[b, :, h * H:(h + 1) * H], res[p][h * C:(h + 1) * C, :]).then_inc(done[f"stored{p}"], 16)

            load(xa, "xa_in", 0, 0)
            sp.dma_start(cst[:, :], packed).then_inc(done["loaded_weights"], 16)
            sp.dma_start(wvo[:, :, :, :], w_vo).then_inc(done["loaded_weights"], 16)
            load(xa, "xa_in", 1, 1)
            samples("sync", sp, neighbours, convolve, unit, attend, last=6)
            for p in range(2):
                sp.wait_ge(done[f"stored{p}"], 32 * (B // 2))

        @block.gpsimd
        def _(pool):
            pool.memset(minus_half[:, :], -0.5).then_inc(done["prepared"], 1)
            pool.memset(w1[:, :], 0.0).then_inc(done["prepared"], 1)
            pool.memset(w2[:, :], 0.0).then_inc(done["prepared"], 1)
            pool.wait_ge(done["prepared"], 3)

            def rstd(b, tag):
                pool.wait_ge(done[f"{tag}_veps"], b + 1)
                pool.tensor_tensor(st[tag][:, 13:14], st[tag][:, 12:13], minus_half[:, 0:1], ALU.pow).then_inc(done[f"{tag}_rstd"], 1)

            def attend(b, p):
                yield
                rstd(b, "in")
                yield
                pool.wait_ge(done["q_rec"], b + 1)
                pool.wait_ge(*since("q_T", b))
                pool.tensor_tensor(qn[:, :, :], qe[:, :, :], qrec[:, :].unsqueeze(2).broadcast_to([P, NT * HEADS, D]),
                                   ALU.mult).then_inc(done["q_norm"], 1)

            def unit(b, p):
                yield
                rstd(b, "att")
                yield
                pool.wait_ge(done["att_normed"], b + 1)
                pool.wait_ge(*since("x1_saved", 16 * b))
                pool.wait_ge(*since("y1_ready", b))
                pool.wait_ge(done[f"xu_in{p}"], 16 * (b - p + 2))
                pool.tensor_tensor(x1[:, :], attn[:, :], xu[p][:, :], ALU.add).then_inc(done["x1_ready"], 1)
                yield
                rstd(b, "mid")
                yield
                pool.wait_ge(done["ss_copied"], b + 1)
                pool.wait_ge(*since("rn_T", b))
                pool.wait_ge(*since("selfsim_ready", b))
                pool.tensor_tensor(rn[:, :], ssq[:, :], minus_half[:, :], ALU.pow).then_inc(done["rn_ready"], 1)

            def neighbours(b, p):
                for r in range(NT):
                    n = NT * b + r
                    rows = slice(r * P, (r + 1) * P)
                    yield
                    constant_first(pool, n + 1)
                    pool.wait_ge(done["tile_rest"], n + 1)
                    pool.affine_select(out=rest[r % 2][:, rows], in_=rest[r % 2][:, rows], compare_op=ALU.not_equal,
                                       fill=MARK, base=0, pattern=[[-1, P]], channel_multiplier=1).then_inc(done["tile_marked"], 1)
                    pool.wait_ge(done["tile_marked"], n + 1)
                    pool.wait_ge(*since("half_T", 2 * (n - 1)))
                    pool.tensor_tensor(adj[r % 2][:, :], sim[r % 4][:, :], rest[r % 2][:, :], ALU.subtract).then_inc(done["tile_adj"], 1)

            def convolve(b, p):
                yield
                rstd(b, "g1")
                yield
                rstd(b, "g2")
                yield
                pool.wait_ge(done["y3_ready"], b + 1)
                pool.wait_ge(done[f"x1_back{p}"], 8 * (b - p + 2))
                pool.wait_ge(*since(f"stored{p}", 16 * (b - p)))
                pool.tensor_tensor(res[p][:, :], y3[:, :], x1c[p][:, :], ALU.add).then_inc(done["res_ready"], 1)

            samples("gpsimd", pool, neighbours, convolve, unit, attend)

        @block.scalar
        def _(act):
            act.wait_ge(done["u_ps"], 1)
            act.copy(u[:, :, :], pB[:, 0:HEADS * C].rearrange("c (h o) -> c h o", h=HEADS)).then_inc(done["u_ready"], 1)
            act.wait_ge(done["loaded_weights"], 16 * 2)

            def attend(b, p):
                yield
                act.wait_ge(done["k_max"], b + 1)
                act.wait_ge(*since("ek_T", b))
                act.wait_ge(*since("k_rec", b))
                act.activation(ek[:, :], pA[:, :], ACT.Exp, bias=kstat[:, 0:1], scale=1.0,
                               accum_out=kstat[:, 1:2]).then_inc(done["k_exp"], 1)
                yield
                act.wait_ge(done["yT_ps"], b + 1)
                act.wait_ge(*since("ky_ps", b))
                act.copy(yT[:, :, :], pB[:, :].rearrange("p (j q) -> p j q", j=NJ)).then_inc(done["yT_copied"], 1)
                yield
                act.wait_ge(done["ek_T"], b + 1)
                act.copy(ekT[:, :, :], pA[:, :].rearrange("p (t q) -> p t q", t=NT)).then_inc(done["ekT_copied"], 1)
                yield
                act.wait_ge(done["ky_ps"], b + 1)
                act.wait_ge(*since("m_ps", b))
                act.copy(kyT[:, :], pB[:, 0:P]).then_inc(done["ky_copied"], 1)
                yield
                act.wait_ge(done["q_sub"], b + 1)
                act.wait_ge(*since("q_norm", b))
                act.activation(qe[:, :, :], qs[:, :, :], ACT.Exp).then_inc(done["q_exp"], 1)
                yield
                act.wait_ge(done["q_T"], b + 1)
                act.wait_ge(*since("att_ps", b))
                act.copy(qh[:, :], pA[:, :]).then_inc(done["qh_copied"], 1)
                yield
                act.wait_ge(done["att_ps"], b + 1)
                act.wait_ge(*since("att_normed", b))
                act.wait_ge(*since("att_stat", b))
                act.activation(att[:, :], pB[:, :], ACT.Identity, bias=vector("b_out")).then_inc(done["att_copied"], 1)

            def unit(b, p):
                yield
                act.wait_ge(done["att_bias"], b + 1)
                act.wait_ge(*since("x1_ready", b))
                act.activation(attn[:, :], att[:, :], ACT.Identity, bias=st["att"][:, 15:16],
                               scale=st["att"][:, 14:15]).then_inc(done["att_normed"], 1)
                yield
                act.wait_ge(done["y1_ready"], b + 1)
                act.wait_ge(*since("ss_ps", b))
                act.activation(sq[:, :], y1[:, :], ACT.Square).then_inc(done["sq_ready"], 1)
                yield
                act.wait_ge(done["xn_ready"], b + 1)
                act.wait_ge(*since(f"stacked{1 - p}", 16 * 6 * (b + p)))
                act.copy(xhi[:, :], xn[p][:, :]).then_inc(done["hi_ready"], 1)

            def neighbours(b, p):
                yield
                act.wait_ge(done["xt1_ps"], b + 1)
                act.wait_ge(*since("g1_ps", b - 1))
                act.copy(xt1[p][:, :, :, :], pB[:, :].rearrange("p (j h c) -> p j h c", j=NJ, h=2)).then_inc(done["xt1_copied"], 1)
                for r in range(NT):
                    yield
                    act.wait_ge(done["tile_sim_ps"], NT * b + r + 1)
                    act.wait_ge(*since("tile_adj", NT * b + r - 3))
                    act.copy(sim[r % 4][:, :], pS[:, :]).then_inc(done["tile_sim"], 1)

            def transposes(b, p):
                for n in range(2 * (NT - 2)):
                    yield
                    copy_transposed(b, p, n // 2, n % 2)

            def copy_transposed(b, p, r, k):
                if r == 0 and k == 0:
                    act.wait_ge(*since("g2_ps", b - 1))
                act.wait_ge(done["half_T"], 2 * (NT * b + r) + k + 1)
                act.copy(adjT[p][:, NJ * k:NJ * (k + 1), r * P:(r + 1) * P], pT[:, k, :, :]).then_inc(done["half_adjT"], 1)

            def silu_parts(b, tag, src, half, tanh):
                act.wait_ge(done[f"{tag}_bias"], b + 1)
                act.wait_ge(*since({"g1": "y2_ready", "g2": "y3_ready"}[tag], b))
                act.activation(half[:, :], src[:, :], ACT.Identity, bias=st[tag][:, 15:16],
                               scale=st[tag][:, 14:15]).then_inc(done[f"{tag}_half"], 1)
                yield
                act.activation(tanh[:, :], src[:, :], ACT.Tanh, bias=st[tag][:, 15:16],
                               scale=st[tag][:, 14:15]).then_inc(done[f"{tag}_tanh"], 1)

            def convolve(b, p):
                for n in range(4):
                    yield
                    copy_transposed(b, p, NT - 2 + n // 2, n % 2)
                yield
                yield from silu_parts(b, "g1", g, zh, th)
                yield
                act.wait_ge(done["xt2_ps"], b + 1)
                act.wait_ge(*since("g2_ps", b))
                act.copy(xt2[:, :, :, :], pC[:, :].rearrange("p (j h c) -> p j h c", j=NJ, h=2)).then_inc(done["xt2_copied"], 1)
                yield
                yield from silu_parts(b, "g2", g2, zh2, th2)

            samples("scalar", act, neighbours, transposes, convolve, unit, attend)

        @block.vector
        def _(dve):
            dve.wait_ge(done["loaded_weights"], 16 * 2)
            dve.wait_ge(done["prepared"], 3)
            dve.tensor_scalar(mark16[:, :], ident, MARK, None, ALU.mult).then_inc(done["prepared"], 1)
            dve.tensor_copy(ident16[:, :], ident).then_inc(done["prepared"], 1)
            for h in range(2):
                c = slice(h * C, (h + 1) * C)
                dve.tensor_scalar(w1[c, c], const("w_1")[c, :], 1.0 / XSCALE, None, ALU.mult).then_inc(done["prepared"], 1)
                dve.tensor_copy(w2[c, c], const("w_2")[c, :]).then_inc(done["prepared"], 1)

            def stats(b, tag, src, ready, shift=None):
                dve.wait_ge(done[ready], b + 1)
                dve.wait_ge(*since(f"{tag}_aggr", b))
                dve.bn_stats(st[tag][:, 0:6], src).then_inc(done[f"{tag}_stat"], 1)
                constant_first(dve, b + 1, b, b)
                dve.wait_ge(done[f"{tag}_stat"], b + 1)
                dve.wait_ge(*since(f"{tag}_mean_ps", b))
                dve.wait_ge(*since(f"{tag}_sq", b))
                dve.bn_aggr(st[tag][:, 6:8], st[tag][:, 0:6]).then_inc(done[f"{tag}_aggr"], 1)
                if shift is not None:
                    dve.wait_ge(done[f"{tag}_aggr"], b + 1)
                    dve.tensor_tensor(st[tag][:, 6:7], st[tag][:, 6:7], shift, ALU.add).then_inc(done[f"{tag}_mean"], 1)

            def deviation(b, tag, ps):
                dve.wait_ge(done[f"{tag}_mean_ps"], b + 1)
                dve.tensor_scalar(st[tag][:, 8:9], ps[:, 0:1], -1.0, None, ALU.mult)
                dve.tensor_tensor(st[tag][:, 9:10], st[tag][:, 6:7], ps[:, 0:1], ALU.subtract).then_inc(done[f"{tag}_dev"], 1)
                dve.wait_ge(done[f"{tag}_dev"], b + 1)
                dve.wait_ge(*since(f"{tag}_var_ps", b))
                dve.scalar_tensor_tensor(out=st[tag][:, 10:11], in0=st[tag][:, 9:10], scalar=st[tag][:, 9:10],
                                         in1=st[tag][:, 7:8], op0=ALU.mult, op1=ALU.add).then_inc(done[f"{tag}_sq"], 1)

            def variance(b, tag, ps):
                dve.wait_ge(done[f"{tag}_var_ps"], b + 1)
                dve.wait_ge(*since(f"{tag}_rstd", b))
                dve.tensor_scalar(st[tag][:, 12:13], ps[:, 1:2], EPS, None, ALU.add).then_inc(done[f"{tag}_veps"], 1)

            def affine(b, tag, weight, bias, half, shift=None):
                f = 0.5 if half else 1.0
                t = st[tag]
                dve.wait_ge(done[f"{tag}_rstd"], b + 1)
                dve.wait_ge(*since({"att": "att_normed", "g1": "g1_tanh", "g2": "g2_tanh"}[tag], b))
                dve.tensor_scalar(t[:, 14:15], t[:, 13:14], weight, f, ALU.mult, ALU.mult).then_inc(done[f"{tag}_scale"], 1)
                if shift is not None:
                    dve.tensor_tensor(t[:, 16:17], t[:, 8:9], shift, ALU.add)
                else:
                    dve.tensor_copy(t[:, 16:17], t[:, 8:9])
                dve.tensor_scalar(t[:, 17:18], bias, f, None, ALU.mult).then_inc(done[f"{tag}_scale"], 1)
                dve.wait_ge(done[f"{tag}_scale"], 2 * (b + 1))
                dve.scalar_tensor_tensor(out=t[:, 15:16], in0=t[:, 16:17], scalar=t[:, 14:15], in1=t[:, 17:18],
                                         op0=ALU.mult, op1=ALU.add).then_inc(done[f"{tag}_bias"], 1)

            def attend(b, p):
                yield
                dve.wait_ge(done[f"xa_in{p}"], 16 * (b - p + 2))
                dve.wait_ge(*since("in_aggr", b))
                dve.bn_stats(st["in"][:, 0:6], xa[p][:, :]).then_inc(done["in_stat"], 1)
                constant_first(dve, b + 1, b, b)
                dve.wait_ge(done["in_stat"], b + 1)
                dve.wait_ge(*since("in_mean_ps", b))
                dve.wait_ge(*since("in_sq", b))
                dve.bn_aggr(st["in"][:, 6:8], st["in"][:, 0:6]).then_inc(done["in_aggr"], 1)
                yield
                deviation(b, "in", pB)
                yield
                variance(b, "in", pB)
                yield
                dve.wait_ge(done["in_rstd"], b + 1)
                dve.wait_ge(*since("q_ps", b))
                dve.tensor_scalar(y[:, :], xa[p][:, :], st["in"][:, 8:9], st["in"][:, 13:14], ALU.add,
                                  ALU.mult).then_inc(done["y_ready"], 1)
                yield
                dve.wait_ge(done["k_ps"], b + 1)
                dve.tensor_reduce(kstat[:, 0:1], pA[:, :], AX.X, ALU.max, negate=True).then_inc(done["k_max"], 1)
                yield
                dve.wait_ge(done["k_exp"], b + 1)
                dve.reciprocal(kstat[:, 2:3], kstat[:, 1:2]).then_inc(done["k_rec"], 1)
                yield
                dve.wait_ge(done["q_ps"], b + 1)
                q_ps = pA[:, :].rearrange("p (g d) -> p g d", d=D)
                dve.tensor_reduce(qmax[:, :], q_ps, AX.X, ALU.max).then_inc(done["q_max"], 1)
                yield
                dve.wait_ge(done["q_max"], b + 1)
                dve.wait_ge(*since("q_exp", b))
                dve.tensor_tensor(qs[:, :, :], q_ps, qmax[:, :].unsqueeze(2).broadcast_to([P, NT * HEADS, D]),
                                  ALU.subtract).then_inc(done["q_sub"], 1)
                yield
                dve.wait_ge(done["m_ps"], b + 1)
                dve.wait_ge(done["k_rec"], b + 1)
                dve.wait_ge(*since("att_ps", b))
                dve.tensor_scalar(mT[:, :], pB[:, 256:256 + C], kstat[:, 2:3], SCALE, ALU.mult, ALU.mult).then_inc(done["m_copied"], 1)
                yield
                dve.wait_ge(done["q_exp"], b + 1)
                dve.tensor_reduce(qsum[:, :], qe[:, :, :], AX.X, ALU.add).then_inc(done["q_sum"], 1)
                yield
                dve.wait_ge(done["q_sum"], b + 1)
                dve.wait_ge(*since("q_norm", b))
                dve.reciprocal(qrec[:, :], qsum[:, :]).then_inc(done["q_rec"], 1)

            def unit(b, p):
                yield
                stats(b, "att", att[:, :], "att_copied")
                yield
                deviation(b, "att", pB)
                yield
                variance(b, "att", pB)
                yield
                affine(b, "att", vector("gn_weight"), vector("gn_bias"), False)
                yield
                stats(b, "mid", x1[:, :], "x1_ready")
                yield
                deviation(b, "mid", pB)
                yield
                variance(b, "mid", pB)
                yield
                dve.wait_ge(done["mid_rstd"], b + 1)
                dve.wait_ge(*since("xn_ready", b))
                dve.wait_ge(*since("sq_ready", b))
                dve.tensor_scalar(y1[:, :], x1[:, :], st["mid"][:, 8:9], st["mid"][:, 13:14], ALU.add,
                                  ALU.mult).then_inc(done["y1_ready"], 1)
                yield
                dve.wait_ge(done["ss_ps"], b + 1)
                dve.wait_ge(*since("rn_ready", b))
                dve.wait_ge(*since("sn_ready", b))
                dve.tensor_copy(ss[:, :], pB[:, 0:NT])
                dve.tensor_scalar(ssq[:, :], pB[:, 0:NT], 1e-24, 1.0 / SSCALE, ALU.max, ALU.mult).then_inc(done["ss_copied"], 1)
                yield
                dve.wait_ge(done["rn_ready"], b + 1)
                dve.wait_ge(done["ss_copied"], b + 1)
                dve.wait_ge(*since("selfsim_ready", b))
                dve.tensor_tensor(sn[:, :], ss[:, :], rn[:, :], ALU.mult).then_inc(done["sn_ready"], 1)
                yield
                dve.wait_ge(done["rn_T"], b + 1)
                dve.wait_ge(*since("rn_saved", 16 * b))
                dve.tensor_copy(rnT[:, :], pB[0:NT, P:2 * P]).then_inc(done["rnT_copied"], 1)
                yield
                dve.wait_ge(done["rn_back"], 32 * (b + 1))
                dve.wait_ge(*since("xt1_ps", b - 1))
                dve.wait_ge(*since("hi_ready", b - 1))
                dve.tensor_tensor(xn[p][:, :], y1[:, :], rbc[:, :], ALU.mult).then_inc(done["xn_ready"], 1)
                yield
                dve.wait_ge(done["hi_ready"], b + 1)
                dve.wait_ge(done["xn_ready"], b + 1)
                dve.wait_ge(*since(f"stacked{1 - p}", 16 * 6 * (b + p)))
                dve.tensor_tensor(xlo[:, :], xn[p][:, :], xhi[:, :], ALU.subtract).then_inc(done["lo_ready"], 1)
                yield
                dve.wait_ge(done["sn_ready"], b + 1)
                dve.wait_ge(*since("v_tot", b - 1))
                dve.tensor_tensor(selfsim[p][:, :], sn[:, :], rn[:, :], ALU.mult).then_inc(done["selfsim_ready"], 1)

            def neighbours(b, p):
                for r in range(NT):
                    n = NT * b + r
                    yield
                    constant_first(dve, n + 1, b)
                    dve.wait_ge(done["tile_sim"], n + 1)
                    dve.wait_ge(*since("v_sum", b))
                    dve.max(top[:, r, :], sim[r % 4][:, :]).then_inc(done["tile_top"], 1)
                    yield
                    constant_first(dve, n + 1, n - 1)
                    dve.wait_ge(done["tile_top"], n + 1)
                    dve.wait_ge(*since("tile_adj", n - 1))
                    dve.match_replace(out=rest[r % 2][:, :], in_to_replace=top[:, r, :], in_values=sim[r % 4][:, :],
                                      imm_value=0.0).then_inc(done["tile_rest"], 1)
                yield
                dve.tensor_reduce(vsum[:, :], top[:, :, :], AX.X, ALU.add).then_inc(done["v_sum"], 1)
                dve.wait_ge(done["v_sum"], b + 1)
                dve.wait_ge(done["selfsim_ready"], b + 1)
                dve.scalar_tensor_tensor(out=vtot[:, :], in0=vsum[:, :], scalar=1e-6 * SSCALE, in1=selfsim[p][:, :],
                                         op0=ALU.add, op1=ALU.add).then_inc(done["v_tot"], 1)
                dve.wait_ge(done["v_tot"], b + 1)
                dve.wait_ge(*since("v_T", b - 1))
                dve.reciprocal(vrec[p][:, :], vtot[:, :]).then_inc(done["v_rec"], 1)

            def gcn(b, tag, first, dst, tanh, half, act_out, act_name, bias, gamma, beta):
                yield
                dve.wait_ge(done[f"{tag}_ps"], b + 1)
                dve.wait_ge(done["v_back"], 32 * (b + 1))
                dve.wait_ge(*since(f"{tag}_tanh", b))
                dve.wait_ge(*since(f"{tag}_stat", b))
                dve.tensor_tensor(dst[:, :], pC[:, :], vbc[:, :], ALU.mult).then_inc(done[f"{tag}_copied"], 1)
                yield
                stats(b, tag, dst[:, :], f"{tag}_copied", shift=vector(bias))
                yield
                deviation(b, tag, pC)
                yield
                variance(b, tag, pC)
                yield
                affine(b, tag, vector(gamma), vector(beta), True, shift=vector(bias))
                yield
                dve.wait_ge(done[f"{tag}_tanh"], b + 1)
                if tag == "g1":
                    dve.wait_ge(*since("xt2_ps", b))
                else:
                    dve.wait_ge(*since("res_ready", b))
                dve.scalar_tensor_tensor(out=act_out[:, :], in0=tanh[:, :], scalar=1.0, in1=half[:, :], op0=ALU.add,
                                         op1=ALU.mult).then_inc(done[act_name], 1)

            def convolve(b, p):
                yield
                dve.wait_ge(done["v_T"], b + 1)
                dve.wait_ge(*since("v_saved", 16 * b))
                dve.tensor_copy(vrT[:, :], pC[0:NT, 0:P]).then_inc(done["vT_copied"], 1)
                yield from gcn(b, "g1", 12, g, th, zh, y2, "y2_ready", "b1", "gamma1", "beta1")
                yield from gcn(b, "g2", 28, g2, th2, zh2, y3, "y3_ready", "b2", "gamma2", "beta2")

            samples("vector", dve, neighbours, convolve, unit, attend)

        @block.tensor
        def _(pe):
            pe.wait_ge(done["loaded_weights"], 16 * 2)
            pe.wait_ge(done["prepared"], PREPARED)
            for h in range(HEADS):
                for c in (slice(0, C), slice(C, P)):
                    mm = pe.matmul(pB[c, h * C:(h + 1) * C], wvo[:, 0, h, :], wvo[:, 1, h, :], start=True, stop=True)
            mm.then_inc(done["u_ps"], 1)
            pe.wait_ge(done["u_ready"], 1)

            def average(b, tag, ps, avg, mean_ready):
                pe.wait_ge(done[mean_ready], b + 1)
                pe.matmul(ps[:, 0:1], const(avg), st[tag][:, 6:7], start=True, stop=True).then_inc(done[f"{tag}_mean_ps"], 1)

            def average_sq(b, tag, ps, avg):
                pe.wait_ge(done[f"{tag}_sq"], b + 1)
                pe.matmul(ps[:, 1:2], const(avg), st[tag][:, 10:11], start=True, stop=True).then_inc(done[f"{tag}_var_ps"], 1)

            def token_block(t):
                h, j = divmod(t, NJ)
                return slice(h * C, (h + 1) * C), slice(j * P, (j + 1) * P)

            def attend(b, p):
                yield
                pe.wait_ge(*since("att_veps", b))
                average(b, "in", pB, "avg_pair", "in_aggr")
                yield
                average_sq(b, "in", pB, "avg_pair")
                yield
                pe.wait_ge(done["y_ready"], b + 1)
                pe.wait_ge(*since("qh_copied", b))
                for h in range(2):
                    c = slice(h * C, (h + 1) * C)
                    mm = pe.matmul(pA[:, h * H:(h + 1) * H], const("w_k")[c, :], y[c, :], start=True, stop=True)
                mm.then_inc(done["k_ps"], 1)
                yield
                pe.wait_ge(done["y_ready"], b + 1)
                pe.wait_ge(*since("mid_veps", b))
                for j in range(NJ):
                    mm = pe.transpose(pB[:, j * P:(j + 1) * P], y[:, j * P:(j + 1) * P], ident)
                mm.then_inc(done["yT_ps"], 1)
                yield
                pe.wait_ge(done["k_exp"], b + 1)
                for t in range(NT):
                    mm = pe.transpose(pA[:, t * P:(t + 1) * P], ek[:, t * P:(t + 1) * P], ident)
                mm.then_inc(done["ek_T"], 1)
                yield
                pe.wait_ge(done["ekT_copied"], b + 1)
                for t in range(NT):
                    c, tok = token_block(t)
                    mm = pe.matmul(pA[:, t * P:(t + 1) * P], y[c, tok], const("w_q")[c, :], start=True, stop=True)
                mm.then_inc(done["q_ps"], 1)
                yield
                pe.wait_ge(done["yT_copied"], b + 1)
                pe.wait_ge(*since("rnT_copied", b))
                for j in range(NJ):
                    for h in range(2):
                        c = slice(h * C, (h + 1) * C)
                        mm = pe.matmul(pB[c, 0:P], yT[:, j, c], ekT[:, h * NJ + j, :], start=(j == 0), stop=(j == NJ - 1))
                mm.then_inc(done["ky_ps"], 1)
                yield
                constant_first(pe, b + 1)
                pe.wait_ge(done["ky_copied"], b + 1)
                for h in range(HEADS):
                    mm = pe.matmul(pB[h * D:(h + 1) * D, 256:256 + C], kyT[:, h * D:(h + 1) * D], u[:, h, :], start=True, stop=True)
                mm.then_inc(done["m_ps"], 1)
                yield
                pe.wait_ge(done["q_norm"], b + 1)
                for t in range(NT):
                    mm = pe.transpose(pA[:, t * P:(t + 1) * P], qn[:, t * HEADS:(t + 1) * HEADS, :], ident)
                mm.then_inc(done["q_T"], 1)
                yield
                pe.wait_ge(done["qh_copied"], b + 1)
                pe.wait_ge(done["m_copied"], b + 1)
                for h in range(2):
                    mm = pe.matmul(pB[h * C:(h + 1) * C, :], mT[:, :], qh[:, h * H:(h + 1) * H], start=True, stop=True)
                mm.then_inc(done["att_ps"], 1)

            def unit(b, p):
                yield
                pe.wait_ge(*since("xt1_copied", b))
                average(b, "att", pB, "avg_sample", "att_aggr")
                yield
                average_sq(b, "att", pB, "avg_sample")
                yield
                pe.wait_ge(done["in_veps"], of_next(b, 1))
                average(b, "mid", pB, "avg_pair", "mid_aggr")
                yield
                average_sq(b, "mid", pB, "avg_pair")
                yield
                pe.wait_ge(done["sq_ready"], b + 1)
                pe.wait_ge(done["yT_copied"], of_next(b, 1))
                for j in range(NJ):
                    mm = pe.matmul(pB[:, j:j + NJ + 1:NJ], sq[:, j * P:(j + 1) * P], const("halves"), start=True, stop=True)
                mm.then_inc(done["ss_ps"], 1)
                yield
                pe.wait_ge(done["rn_ready"], b + 1)
                pe.transpose(pB[0:NT, P:2 * P], rn[:, :], ident).then_inc(done["rn_T"], 1)

            def neighbours(b, p):
                yield
                pe.wait_ge(done["xn_ready"], b + 1)
                pe.wait_ge(done["att_copied"], of_next(b, 1))
                for j in range(NJ):
                    mm = pe.matmul(pB[:, j * P:(j + 1) * P], xn[p][:, j * P:(j + 1) * P], w1[:, :], start=True, stop=True)
                mm.then_inc(done["xt1_ps"], 1)
                pe.wait_ge(done[f"stacked{p}"], 16 * 6 * (b - p + 2))
                for r in range(NT):
                    yield
                    pe.wait_ge(*since("tile_sim", NT * b + r))
                    rows = slice(r * P, (r + 1) * P)
                    for h in range(2):
                        tok = slice(h * H, (h + 1) * H)
                        pe.matmul(pS[:, tok], hilo[p][:, rows], hihi[p][:, tok], start=True, stop=False)
                        if r // NJ == h:
                            pe.matmul(pS[:, rows], ident16[:, :], mark16[:, :], start=False, stop=False,
                                      skip_group_check=True)
                        mm = pe.matmul(pS[:, tok], hilo[p][:, rows], lolo[p][:, tok], start=False, stop=True)
                    mm.then_inc(done["tile_sim_ps"], 1)

            def transposes(b, p):
                for n in range(2 * (NT - 2)):
                    yield
                    transpose_half(b, n // 2, n % 2)

            def transpose_half(b, r, k):
                pe.wait_ge(done["tile_adj"], NT * b + r + 1)
                pe.wait_ge(*since("half_adjT", 2 * (NT * b + r) + k - 1))
                for j in range(NJ):
                    t = NJ * k + j
                    mm = pe.transpose(pT[:, k, j, :], adj[r % 2][:, t * P:(t + 1) * P], ident)
                mm.then_inc(done["half_T"], 1)

            def aggregate(xt, p, first, signal):
                for t in range(NT):
                    yield
                    for h in range(2):
                        mm = pe.matmul(pC[h * C:(h + 1) * C, :], xt[:, t % NJ, t // NJ, :], adjT[p][:, t, h * H:(h + 1) * H],
                                       start=(t == 0), stop=(t == NT - 1))
                mm.then_inc(done[signal], 1)

            def convolve(b, p):
                for n in range(4):
                    yield
                    transpose_half(b, NT - 2 + n // 2, n % 2)
                yield
                pe.wait_ge(done["v_rec"], b + 1)
                pe.wait_ge(*since("g2_veps", b))
                pe.transpose(pC[0:NT, 0:P], vrec[p][:, :], ident).then_inc(done["v_T"], 1)
                yield
                pe.wait_ge(done["vT_copied"], b + 1)
                pe.wait_ge(done["xt1_copied"], b + 1)
                pe.wait_ge(done["half_adjT"], 2 * NT * (b + 1))
                yield from aggregate(xt1[p], p, 4, "g1_ps")
                yield
                pe.wait_ge(done["g1_copied"], b + 1)
                average(b, "g1", pC, "avg_group", "g1_mean")
                yield
                average_sq(b, "g1", pC, "avg_group")
                yield
                pe.wait_ge(done["y2_ready"], b + 1)
                pe.wait_ge(done["g1_veps"], b + 1)
                for j in range(NJ):
                    mm = pe.matmul(pC[:, j * P:(j + 1) * P], y2[:, j * P:(j + 1) * P], w2[:, :], start=True, stop=True)
                mm.then_inc(done["xt2_ps"], 1)
                yield
                pe.wait_ge(done["xt2_copied"], b + 1)
                yield from aggregate(xt2, p, 20, "g2_ps")
                yield
                pe.wait_ge(done["g2_copied"], b + 1)
                average(b, "g2", pC, "avg_group", "g2_mean")
                yield
                average_sq(b, "g2", pC, "avg_group")

            samples("tensor", pe, neighbours, transposes, convolve, unit, attend)


def kernel(**inputs):
    import concourse.bacc as bacc
    from concourse.bass_utils import run_bass_kernel_spmd as run

    a = {n: np.asarray(v) for n, v in inputs.items()}
    x = a["x"]
    B, C, Hh, Ww = x.shape
    w_qkv = a["L0_conv_w_qkv"]
    hid = w_qkv.shape[0] // 3

    def twice(m):
        return np.concatenate([m, m], axis=0)

    cols = [a["L0_conv_b_out"], a["L0_conv_gn_weight"], a["L0_conv_gn_bias"], a["L1_conv_b1"], a["L1_conv_gamma1"],
            a["L1_conv_beta1"], a["L1_conv_b2"], a["L1_conv_gamma2"], a["L1_conv_beta2"]]
    arrays = {
        "x": np.ascontiguousarray(x.reshape(B, C, Hh * Ww)),
        "packed": np.ascontiguousarray(np.concatenate(
            [shape_constants(C)] + [twice(m) for m in (w_qkv[0:hid].T, w_qkv[hid:2 * hid].T, a["L1_conv_w1"], a["L1_conv_w2"],
                                                       np.stack(cols, axis=1))], axis=1)),
        "w_vo": np.ascontiguousarray(np.stack([m.reshape(HEADS, -1, C).transpose(1, 0, 2)
                                               for m in (w_qkv[2 * hid:], a["L0_conv_w_out"].T)], axis=1)),
    }
    nc = bacc.Bacc("TRN2", target_bir_lowering=False, num_devices=1)
    args = [nc.dram_tensor(n, v.shape, mybir.dt.from_np(v.dtype), kind="ExternalInput").ap() for n, v in arrays.items()]
    out = nc.dram_tensor("out", (B, C, Hh * Ww), F32, kind="ExternalOutput").ap()
    build(nc, *args, out)
    r = run(nc, [arrays], core_ids=[0])
    return r.results[0]["out"].reshape(B, C, Hh, Ww)
```
